# Optimizing a Trainium2 kernel written in Bass

```python
import numpy as np
import jax
import jax.numpy as jnp

def _softmax(x, axis=-1):
    return jax.nn.softmax(x, axis=axis)

def _gelu(x):
    return jax.nn.gelu(x, approximate=True)

def _silu(x):
    return jax.nn.silu(x)

def _sigmoid(x):
    return jax.nn.sigmoid(x)

def _layernorm(x, axis=-1, eps=1e-05):
    m = jnp.mean(x, axis=axis, keepdims=True)
    v = jnp.var(x, axis=axis, keepdims=True)
    return (x - m) / jnp.sqrt(v + eps)

def _scatter_add(tgt, idx, src, axis=0):
    return tgt.at[idx].add(src)

def _segment_sum(src, seg, n):
    return jax.ops.segment_sum(src, seg, n)
kernel_name = 'mk_decoder_postln_d1_seqx_r8_1e65b5'

def setup_inputs(seed: int=0):
    np.random.seed(seed)
    _w = jnp.asarray

    def _rec_inputs():
        import jax
        import jax.numpy as jnp
        _rk = jax.random.key(seed)
        x = -0.0003929 + 0.9999 * jax.random.normal(jax.random.fold_in(_rk, 1), (4, 512, 128), jnp.float32)
        _lenS = 512 - jax.random.randint(jax.random.fold_in(_rk, 7), (4,), 0, max(1, 512 // 4) + 1, jnp.int32)
        _lenS2 = 77 - jax.random.randint(jax.random.fold_in(_rk, 8), (4,), 0, max(1, 77 // 4) + 1, jnp.int32)
        _ctx_1024P = jax.random.normal(jax.random.fold_in(_rk, 11), (4, 16, 128), jnp.float32)
        _ctx_1024c = jax.random.dirichlet(jax.random.fold_in(_rk, 511), 0.3 * jnp.ones((16,), jnp.float32), (4, 77))
        _ctx_1024t = jnp.einsum('bsk,bkd->bsd', _ctx_1024c, _ctx_1024P)
        _ctx_1024t = _ctx_1024t * jax.lax.rsqrt(jnp.mean(jnp.square(_ctx_1024t)) + 1e-12) * 0.953939
        ctx_1024 = 2.81802e-05 + 1.00001 * (_ctx_1024t + 0.3 * jax.random.normal(jax.random.fold_in(_rk, 611), (4, 77, 128), jnp.float32))
        return (x, ctx_1024)
    x, ctx_1024 = _rec_inputs()

    def _L0_attn_setup():
        import jax, jax.numpy as jnp
        import numpy as np
        S, B, D, H = (256, 2, 128, 16)
        DH = D // H
        WINDOW = 32
        DILATION = 1

        def _causal_window_bias(seq_len, window_len, dilation):
            idx = jnp.arange(seq_len)
            diff = idx[:, None] - idx[None, :]
            allowed = (diff >= 0) & (diff <= dilation * (window_len - 1)) & (diff % dilation == 0)
            return jnp.where(allowed, 0.0, -jnp.inf).astype(jnp.float32)
        key = jax.random.key(seed)
        ks = jax.random.split(key, 10)
        scale = 1.0 / np.sqrt(D)
        x = jax.random.normal(ks[0], (S, B, D), dtype=jnp.float32)
        Wq = jax.random.normal(ks[1], (D, D), dtype=jnp.float32) * scale
        Wk = jax.random.normal(ks[2], (D, D), dtype=jnp.float32) * scale
        Wv = jax.random.normal(ks[3], (D, D), dtype=jnp.float32) * scale
        Wo = jax.random.normal(ks[4], (D, D), dtype=jnp.float32) * scale
        bq = jax.random.normal(ks[5], (D,), dtype=jnp.float32) * 0.01
        bk = jax.random.normal(ks[6], (D,), dtype=jnp.float32) * 0.01
        bv = jax.random.normal(ks[7], (D,), dtype=jnp.float32) * 0.01
        bo = jax.random.normal(ks[8], (D,), dtype=jnp.float32) * 0.01
        beta = jax.random.normal(ks[9], (H,), dtype=jnp.float32) * 0.1
        return {'x': x, 'Wq': Wq, 'bq': bq, 'Wk': Wk, 'bk': bk, 'Wv': Wv, 'bv': bv, 'Wo': Wo, 'bo': bo, 'beta': beta}
    _L0_attn_all = _L0_attn_setup()
    _L0_attn_in = {k: v for k, v in _L0_attn_all.items() if k in ('Wq', 'bq', 'Wk', 'bk', 'Wv', 'bv', 'Wo', 'bo', 'beta')}
    del _L0_attn_all

    def _L0_xattn_setup():
        import jax, jax.numpy as jnp
        import numpy as np
        import math
        B, L, D = (4, 512, 128)
        M = 32
        EPS = 1e-06
        key = jax.random.key(seed)
        kq, kk, kv, kp = jax.random.split(key, 4)
        Q = jax.random.normal(kq, (B, L, D), dtype=jnp.float32)
        K = jax.random.normal(kk, (B, L, D), dtype=jnp.float32)
        V = jax.random.normal(kv, (B, L, D), dtype=jnp.float32)
        projection = jax.random.normal(kp, (M, D), dtype=jnp.float32)
        return {'Q': Q, 'K': K, 'V': V, 'projection': projection}
    _L0_xattn_all = _L0_xattn_setup()
    _L0_xattn_in = {k: v for k, v in _L0_xattn_all.items() if k in ('projection',)}
    del _L0_xattn_all

    def _L0_ffn_setup():
        import jax, jax.numpy as jnp
        import numpy as np
        H = 128
        I = 256
        E = 8
        B, S = (2, 128)

        def _swiglu(x, wg, wu, wd):
            return jax.nn.silu(x @ wg) * (x @ wu) @ wd
        key = jax.random.key(seed)
        ks = jax.random.split(key, 8)
        sc_h = 1.0 / np.sqrt(H)
        sc_i = 1.0 / np.sqrt(I)
        return {'hidden_states': jax.random.normal(ks[0], (B, S, H), jnp.float32), 'gate_w': jax.random.normal(ks[1], (H, E), jnp.float32) * sc_h, 'sh_gate': jax.random.normal(ks[2], (H, I), jnp.float32) * sc_h, 'sh_up': jax.random.normal(ks[3], (H, I), jnp.float32) * sc_h, 'sh_down': jax.random.normal(ks[4], (I, H), jnp.float32) * sc_i, 'rt_gate': jax.random.normal(ks[5], (E, H, I), jnp.float32) * sc_h, 'rt_up': jax.random.normal(ks[6], (E, H, I), jnp.float32) * sc_h, 'rt_down': jax.random.normal(ks[7], (E, I, H), jnp.float32) * sc_i}
    _L0_ffn_all = _L0_ffn_setup()
    _L0_ffn_in = {k: v for k, v in _L0_ffn_all.items() if k in ('gate_w', 'sh_gate', 'sh_up', 'sh_down', 'rt_gate', 'rt_up', 'rt_down')}
    del _L0_ffn_all
    return {'x': x, 'ctx_1024': ctx_1024, 'L0_attn_Wq': _L0_attn_in['Wq'], 'L0_attn_bq': _L0_attn_in['bq'], 'L0_attn_Wk': _L0_attn_in['Wk'], 'L0_attn_bk': _L0_attn_in['bk'], 'L0_attn_Wv': _L0_attn_in['Wv'], 'L0_attn_bv': _L0_attn_in['bv'], 'L0_attn_Wo': _L0_attn_in['Wo'], 'L0_attn_bo': _L0_attn_in['bo'], 'L0_attn_beta': _L0_attn_in['beta'], 'L0_xattn_projection': _L0_xattn_in['projection'], 'L0_ffn_gate_w': _L0_ffn_in['gate_w'], 'L0_ffn_sh_gate': _L0_ffn_in['sh_gate'], 'L0_ffn_sh_up': _L0_ffn_in['sh_up'], 'L0_ffn_sh_down': _L0_ffn_in['sh_down'], 'L0_ffn_rt_gate': _L0_ffn_in['rt_gate'], 'L0_ffn_rt_up': _L0_ffn_in['rt_up'], 'L0_ffn_rt_down': _L0_ffn_in['rt_down']}

def reference(x, ctx_1024, L0_attn_Wq, L0_attn_bq, L0_attn_Wk, L0_attn_bk, L0_attn_Wv, L0_attn_bv, L0_attn_Wo, L0_attn_bo, L0_attn_beta, L0_xattn_projection, L0_ffn_gate_w, L0_ffn_sh_gate, L0_ffn_sh_up, L0_ffn_sh_down, L0_ffn_rt_gate, L0_ffn_rt_up, L0_ffn_rt_down):
    import jax
    import jax.numpy as jnp

    def _L0_attn_ref(x, Wq, bq, Wk, bk, Wv, bv, Wo, bo, beta):
        import jax, jax.numpy as jnp
        import numpy as np
        S, B, D, H = (256, 2, 128, 16)
        DH = D // H
        WINDOW = 32
        DILATION = 1

        def _causal_window_bias(seq_len, window_len, dilation):
            idx = jnp.arange(seq_len)
            diff = idx[:, None] - idx[None, :]
            allowed = (diff >= 0) & (diff <= dilation * (window_len - 1)) & (diff % dilation == 0)
            return jnp.where(allowed, 0.0, -jnp.inf).astype(jnp.float32)
        s, b, d = x.shape
        q = x @ Wq.T + bq
        k = x @ Wk.T + bk
        v = x @ Wv.T + bv
        q = q.reshape(s, b, H, DH).transpose(1, 2, 0, 3)
        k = k.reshape(s, b, H, DH).transpose(1, 2, 0, 3)
        v = v.reshape(s, b, H, DH).transpose(1, 2, 0, 3)
        q = q / (np.sqrt(DH) * jnp.exp(beta)[None, :, None, None])
        bias = _causal_window_bias(s, WINDOW, DILATION)
        scores = jnp.einsum('bhqd,bhkd->bhqk', q, k) + bias[None, None]
        p = jax.nn.softmax(scores, axis=-1)
        out = jnp.einsum('bhqk,bhkd->bhqd', p, v)
        out = out.transpose(2, 0, 1, 3).reshape(s, b, d)
        return out @ Wo.T + bo

    def _L0_xattn_ref(Q, K, V, projection):
        import jax, jax.numpy as jnp
        import numpy as np
        import math
        B, L, D = (4, 512, 128)
        M = 32
        EPS = 1e-06
        d_model = Q.shape[-1]
        m = projection.shape[0]
        inv_sqrt_d = 1.0 / math.sqrt(d_model)
        rf_q = jnp.exp(jnp.einsum('bld,md->blm', Q * inv_sqrt_d, projection)) / math.sqrt(m)
        rf_k = jnp.exp(jnp.einsum('bld,md->blm', K * inv_sqrt_d, projection))
        KV = jnp.einsum('blm,bld->bmd', rf_k, V)
        Z = jnp.sum(rf_k, axis=1)
        out = jnp.einsum('blm,bmd->bld', rf_q, KV)
        normalizer = jnp.einsum('blm,bm->bl', rf_q, Z) + EPS
        return out / normalizer[..., None]

    def _L0_ffn_ref(hidden_states, gate_w, sh_gate, sh_up, sh_down, rt_gate, rt_up, rt_down):
        import jax, jax.numpy as jnp
        import numpy as np
        H = 128
        I = 256
        E = 8
        B, S = (2, 128)

        def _swiglu(x, wg, wu, wd):
            return jax.nn.silu(x @ wg) * (x @ wu) @ wd
        b, s, h = hidden_states.shape
        x = hidden_states.reshape(-1, h)
        logits = x @ gate_w
        top_val = jnp.max(logits, axis=-1, keepdims=True)
        top_id = jnp.argmax(logits, axis=-1)
        score = jax.nn.sigmoid(top_val)
        xs = x * score
        g = jnp.einsum('th,ehi->eti', xs, rt_gate)
        u = jnp.einsum('th,ehi->eti', xs, rt_up)
        act = jax.nn.silu(g) * u
        y = jnp.einsum('eti,eih->eth', act, rt_down)
        onehot = jax.nn.one_hot(top_id, E, dtype=x.dtype)
        routed = jnp.einsum('eth,te->th', y, onehot)
        shared = _swiglu(x, sh_gate, sh_up, sh_down)
        return (shared + routed).reshape(b, s, h)
    x = _layernorm(x + _L0_attn_ref(x, L0_attn_Wq, L0_attn_bq, L0_attn_Wk, L0_attn_bk, L0_attn_Wv, L0_attn_bv, L0_attn_Wo, L0_attn_bo, L0_attn_beta), axis=-1)
    x = _layernorm(x + _L0_xattn_ref(x, ctx_1024, ctx_1024, L0_xattn_projection), axis=-1)
    x = _layernorm(x + _L0_ffn_ref(x, L0_ffn_gate_w, L0_ffn_sh_gate, L0_ffn_sh_up, L0_ffn_sh_down, L0_ffn_rt_gate, L0_ffn_rt_up, L0_ffn_rt_down), axis=-1)
    return x

_drawn_inputs = setup_inputs


def setup_inputs(seed=0):
    import zlib

    import numpy as np

    out = dict(_drawn_inputs(seed))
    spreads = {}
    factors = {'L0_attn_bq': 4.32, 'L0_attn_bk': 8.0, 'L0_attn_bo': 2.785}
    for name, (base, spread) in spreads.items():
        noise = np.random.default_rng([zlib.crc32(name.encode()), seed]).standard_normal(out[name].shape)
        drawn = base * np.exp(spread * noise) if base else spread * noise
        out[name] = jnp.asarray(drawn.astype(out[name].dtype))
    for name, factor in factors.items():
        out[name] = (out[name] * factor).astype(out[name].dtype)
    return out
```

```python
import math
from contextlib import ExitStack

import numpy as np

import concourse.bass as bass
from concourse import mybir


def build_decoder(nc, t):
    F32 = mybir.dt.float32
    BF16 = mybir.dt.bfloat16
    I32 = mybir.dt.int32
    ALU = mybir.AluOpType
    ACT = mybir.ActivationFunctionType
    X = mybir.AxisListType.X
    ds = bass.ds

    P = 128
    S, BATCH, D = t["x"].shape
    NC = BATCH // P
    TOK = S * BATCH
    HEADS, DH = 16, D // 16
    CTX = t["ctx_1024"].shape[1]
    M = t["L0_xattn_projection"].shape[0]
    E, _, I = t["L0_ffn_rt_gate"].shape
    HALVES = I // P
    PAIRS = S * (S + 1) // 2 - 1
    PB = [0, 0, 2, 5]
    EPS_LN, EPS_X = 1e-5, 1e-6
    INV_SQRT_D = 1.0 / math.sqrt(D)
    INV_SQRT_DH = 1.0 / math.sqrt(DH)
    NB = TOK // P + E - 1
    ROWS = TOK + P
    FILLER = E * ROWS
    AW = D + 1
    BW = D + 1
    NOTOK = 1 << 20
    KB = TOK // P
    RING = 4

    x_in = t["x"].rearrange("s (c p) d -> c p s d", p=P)
    out_rows = t["out"].rearrange("s b d -> (s b) d")

    ctx = ExitStack()
    with ctx:
        def sb(name, shape, dt=F32):
            return ctx.enter_context(nc.sbuf_tensor(name, shape, dt))

        def sem(name):
            return ctx.enter_context(nc.semaphore(name))

        table_a = nc.dram_tensor("table_a", (FILLER + P, AW), F32, kind="Internal").ap()
        table_b = nc.dram_tensor("table_b", (FILLER + P, BW), F32, kind="Internal").ap()

        ident = sb("ident", [P, P])
        before = sb("before", [P, P], BF16)
        ones16 = sb("ones16", [P, P], BF16)
        rev = sb("rev", [P, E])
        region = sb("region", [P, E])
        kcol = sb("kcol", [1, KB])
        bcol = sb("bcol", [1, NB])
        upto = sb("upto", [1, E * E])
        eps_ln = sb("eps_ln", [P, 1])
        mhalf = sb("mhalf", [P, S])
        filler_a = sb("filler_a", [P, AW])
        filler_b = sb("filler_b", [P, BW])
        w_nat = sb("w_nat", [P, 4 * P])
        w_t = sb("w_t", [P, 4 * P])
        bias = sb("bias", [P, 4 * P])
        beta = sb("beta", [P, HEADS])
        qscale = sb("qscale", [P, HEADS])
        proj = sb("proj", [M, D])
        proj_t = sb("proj_t", [D, M])
        ctx1 = sb("ctx1", [CTX, S * (D + 1)])
        ctx_t = sb("ctx_t", [D, S * CTX])
        rf_k = sb("rf_k", [CTX, S * M])
        kvz = sb("kvz", [M, S * (D + 1)])
        gate = sb("gate", [D, E])
        sh_gu = sb("sh_gu", [D, 2 * I])
        sh_dn = sb("sh_dn", [P, HALVES * D])
        rt_gu = sb("rt_gu", [D, E * 2 * I])
        rt_dn = sb("rt_dn", [P, E * HALVES * D])

        CW = S * D
        x0 = sb("x0", [P, NC * CW])
        xb = sb("xb", [P, NC * CW])
        x0_t = sb("x0_t", [P, NC * CW])
        qkv = sb("qkv", [P, NC * S * 3 * D])
        pq = sb("pq", [P, PAIRS * D])
        SW = (S - 1) * S * HEADS
        score = sb("score", [P, NC * SW])
        smax = sb("smax", [P, NC * (S - 1) * HEADS])
        ssub = sb("ssub", [P, NC * SW])
        prob = sb("prob", [P, NC * SW])
        ssum = sb("ssum", [P, NC * (S - 1) * HEADS])
        srec = sb("srec", [P, NC * (S - 1) * HEADS])
        pv = sb("pv", [P, PAIRS * D])
        att = sb("att", [P, NC * (S - 1) * D])
        att_t = sb("att_t", [P, CW])
        r1 = sb("r1", [P, CW])
        r2 = sb("r2", [P, CW])
        st = sb("st", [P, NC * 2 * S * 6])
        mv = sb("mv", [P, NC * 2 * S * 2])
        ve = sb("ve", [P, NC * 2 * S])
        rs = sb("rs", [P, NC * 2 * S])
        x1 = sb("x1", [P, NC * CW])
        x1_t = sb("x1_t", [P, CW])
        rf_q = sb("rf_q", [M, CW])
        den = sb("den", [P, NC * S])
        rden = sb("rden", [P, NC * S])
        row_a = sb("row_a", [P, NC * S * AW])
        x2_t = sb("x2_t", [P, CW])
        th = sb("th", [P, HALVES * CW])
        hg = sb("hg", [P, HALVES * CW])
        hid = sb("hid", [P, HALVES * CW])
        row_b = sb("row_b", [P, NC * S * BW])
        ltop = sb("ltop", [P, NC * S])
        leq = sb("leq", [P, NC * S * E])
        lcand = sb("lcand", [P, NC * S * E])
        lfirst = sb("lfirst", [P, NC * S])
        hot = sb("hot", [P, NC * S * E], BF16)
        cum = sb("cum", [P, (NC * S + 1) * E], BF16)
        tsc = sb("tsc", [P, NC * S])
        rk = sb("rk", [P, NC * S * E])
        rkh = sb("rkh", [P, NC * S * E])
        pos = sb("pos", [P, NC * S], I32)

        cnt = sb("cnt", [1, E])
        gtk = sb("gtk", [1, E * KB])
        nblk = sb("nblk", [1, E])
        nmask = sb("nmask", [1, E * E])
        cblk = sb("cblk", [1, E])
        dstep = sb("dstep", [1, E])
        ge = sb("ge", [1, NB * E])
        ged = sb("ged", [1, NB * E])
        esum = sb("esum", [1, NB])
        rsum = sb("rsum", [1, NB])
        radd = sb("radd", [1, NB])
        blk_e = sb("blk_e", [1, NB], I32)
        blk_row = sb("blk_row", [1, NB], I32)
        tail_row = sb("tail_row", [1, E], I32)

        xs = sb("xs", [P, RING * AW])
        bs = sb("bs", [P, RING * BW])
        token = sb("token", [P, RING], I32)
        xs_t = sb("xs_t", [P, 2 * D])
        si = sb("si", [P, 2 * I])
        ac = sb("ac", [P, 2 * I])
        ac_t = sb("ac_t", [P, 2 * I])
        r3 = sb("r3", [P, RING * D])
        st3 = sb("st3", [P, RING * 6])
        mv3 = sb("mv3", [P, RING * 2])
        ve3 = sb("ve3", [P, RING])
        rs3 = sb("rs3", [P, RING])
        fin = sb("fin", [P, RING * D])

        bank = [ctx.enter_context(nc.psum_tensor(f"bank{i}", [P, 512], F32)) for i in range(8)]

        ld_w, ld_bias, ld_beta, ld_ctx, ld_proj, ld_gate = map(
            sem, ["ld_w", "ld_bias", "ld_beta", "ld_ctx", "ld_proj", "ld_gate"])
        ld_x = [sem(f"ld_x{c}") for c in range(NC)]
        ld_sh, ld_rt = sem("ld_sh"), sem("ld_rt")
        k_zero, k_mask, k_const, k_cum0 = sem("k_zero"), sem("k_mask"), sem("k_const"), sem("k_cum0")
        w_ps, w_sb, qs_sb, bq_sb, c_ps, c_sb, fk_ps, fk_sb, kv_ps, kv_sb = map(
            sem, ["w_ps", "w_sb", "qs_sb", "bq_sb", "c_ps", "c_sb", "fk_ps", "fk_sb", "kv_ps", "kv_sb"])
        x0t_ps, x0t_sb, qkv_ps, qkv_sb, pq_sb, xb_sb = map(
            sem, ["x0t_ps", "x0t_sb", "qkv_ps", "qkv_sb", "pq_sb", "xb_sb"])
        score_sb, smax_sb, ssub_sb, exp_sb, ssum_sb, srec_sb, prob_sb, pv_sb, att_sb = map(
            sem, ["score_sb", "smax_sb", "ssub_sb", "exp_sb", "ssum_sb", "srec_sb", "prob_sb", "pv_sb", "att_sb"])
        att_ps, att_t_sb, ao_ps = map(sem, ["att_ps", "att_t_sb", "ao_ps"])
        r1_sb, st1_sb, mv1_sb, ve1_sb, rs1_sb, x1_sb = map(
            sem, ["r1_sb", "st1_sb", "mv1_sb", "ve1_sb", "rs1_sb", "x1_sb"])
        x1t_ps, x1t_sb, fq_ps, fq_sb, xo_ps, den_sb, rden_sb = map(
            sem, ["x1t_ps", "x1t_sb", "fq_ps", "fq_sb", "xo_ps", "den_sb", "rden_sb"])
        r2_sb, st2_sb, mv2_sb, ve2_sb, rs2_sb, x2_sb, x2t_ps, x2t_sb = map(
            sem, ["r2_sb", "st2_sb", "mv2_sb", "ve2_sb", "rs2_sb", "x2_sb", "x2t_ps", "x2t_sb"])
        lg_ps, ltop_sb, leq_sb, lcand_sb, lfirst_sb, hot_sb, cum_sb, tsc_sb, sc_sb, rank_ps, rk_sb, rkh_sb, pos_sb = map(
            sem, ["lg_ps", "ltop_sb", "leq_sb", "lcand_sb", "lfirst_sb", "hot_sb", "cum_sb", "tsc_sb", "sc_sb",
                  "rank_ps", "rk_sb", "rkh_sb", "pos_sb"])
        scat_a, scat_b, fill_a, fill_b = map(sem, ["scat_a", "scat_b", "fill_a", "fill_b"])
        g_ps, th_sb, hg_sb, hid_sb, sy_ps, rowb_sb = map(
            sem, ["g_ps", "th_sb", "hg_sb", "hid_sb", "sy_ps", "rowb_sb"])
        cnt_ps, tab = sem("cnt_ps"), sem("tab")
        ld_xs = [sem(f"ld_xs{q}") for q in range(RING)]
        ld_bs = [sem(f"ld_bs{q}") for q in range(RING)]
        xst_ps, xst_sb, gu_ps, si_sb, ac_sb, act_ps, act_sb, y_ps = map(
            sem, ["xst_ps", "xst_sb", "gu_ps", "si_sb", "ac_sb", "act_ps", "act_sb", "y_ps"])
        r3_sb, st3_sb, mv3_sb, ve3_sb, rs3_sb, fin_sb = map(
            sem, ["r3_sb", "st3_sb", "mv3_sb", "ve3_sb", "rs3_sb", "fin_sb"])
        out_dma = [sem(f"out_dma{q}") for q in range(RING)]

        TAB = 13

        def tile_of(buf, c, s, w=D, row=None):
            row = w if row is None else row
            return buf[:, ds((c * S + s) * row, w)]

        def chunk_of(buf, c, w):
            return buf[:, ds(c * w, w)]

        def qkv_part(c, s, part, n=1):
            v = qkv[:, ds((c * S + s) * 3 * D, n * 3 * D)].rearrange("p (j w) -> p j w", w=3 * D)
            return v[:, :, part * D:(part + 1) * D]

        block = ctx.enter_context(nc.Block())

        @block.sync
        def _(sp):
            sp.dma_start(x0[:, 0:CW].rearrange("p (s d) -> p s d", s=S), x_in[0]).then_inc(ld_x[0], 16)
            for n, w in enumerate(("Wq", "Wk", "Wv", "Wo")):
                sp.dma_start(w_nat[:, n * P:(n + 1) * P], t[f"L0_attn_{w}"]).then_inc(ld_w, 16)
            for c in range(1, NC):
                sp.dma_start(x0[:, c * CW:(c + 1) * CW].rearrange("p (s d) -> p s d", s=S), x_in[c]).then_inc(ld_x[c], 16)
            sp.dma_start(sh_gu[:, 0:I], t["L0_ffn_sh_gate"]).then_inc(ld_sh, 16)
            sp.dma_start(sh_gu[:, I:2 * I], t["L0_ffn_sh_up"]).then_inc(ld_sh, 16)
            sp.dma_start(sh_dn[:].rearrange("p (h d) -> p h d", h=HALVES),
                         t["L0_ffn_sh_down"].rearrange("(h p) d -> p h d", p=P)).then_inc(ld_sh, 16)
            gu = rt_gu[:].rearrange("p (e i) -> p e i", e=E)
            sp.dma_start(gu[:, :, 0:I], t["L0_ffn_rt_gate"].rearrange("e h i -> h e i")).then_inc(ld_rt, 16)
            sp.dma_start(gu[:, :, I:2 * I], t["L0_ffn_rt_up"].rearrange("e h i -> h e i")).then_inc(ld_rt, 16)
            sp.dma_start(rt_dn[:].rearrange("p (e h d) -> p e h d", e=E, h=HALVES),
                         t["L0_ffn_rt_down"].rearrange("e (h p) d -> p e h d", p=P)).then_inc(ld_rt, 16)
            sp.wait_ge(k_const, 1)
            sp.dma_start(table_a[FILLER:FILLER + P, :], filler_a[:]).then_inc(fill_a, 16)
            sp.dma_start(table_b[FILLER:FILLER + P, :], filler_b[:]).then_inc(fill_b, 16)

            sp.wait_ge(tab, TAB)
            for e in range(E):
                row = sp.value_load(tail_row[0:1, e:e + 1], min_val=e * ROWS, max_val=e * ROWS + TOK)
                sp.dma_start(table_a[ds(row, P), :], filler_a[:]).then_inc(fill_a, 16)
            for e in range(E):
                row = sp.value_load(tail_row[0:1, e:e + 1], min_val=e * ROWS, max_val=e * ROWS + TOK)
                sp.dma_start(table_b[ds(row, P), :], filler_b[:]).then_inc(fill_b, 16)

            def load_a(b, q, used=None):
                row = sp.value_load(blk_row[0:1, ds(b, 1)], min_val=0, max_val=FILLER)
                if used is not None:
                    sp.wait_ge(ac_sb, used)
                sp.dma_start(xs[:, q * AW:(q + 1) * AW], table_a[ds(row, P), :]).then_inc(ld_xs[q], 16)

            def load_b(b, q, used=None):
                row = sp.value_load(blk_row[0:1, ds(b, 1)], min_val=0, max_val=FILLER)
                if used is not None:
                    sp.wait_ge(r3_sb, used)
                sp.dma_start(bs[:, q * BW:(q + 1) * BW], table_b[ds(row, P), :]).then_inc(ld_bs[q], 16)

            sp.wait_ge(scat_a, 16 * NC * S)
            sp.wait_ge(fill_a, 16 * (E + 1))
            for b in range(RING):
                load_a(b, b)
            sp.wait_ge(scat_b, 16 * NC * S)
            sp.wait_ge(fill_b, 16 * (E + 1))
            for b in range(RING):
                load_b(b, b)
            LOOPS = (NB - RING) // RING
            with sp.Fori(0, LOOPS) as k:
                for q in range(RING):
                    load_a(RING * k + RING + q, q, RING * k + q + 1)
                    load_b(RING * k + RING + q, q, RING * k + q + 1)
            for b in range(RING * (LOOPS + 1), NB):
                q = b % RING
                load_a(b, q, b - RING + 1)
                load_b(b, q, b - RING + 1)
            for q in range(RING):
                sp.wait_ge(out_dma[q], 16 * ((NB - 1 - q) // RING + 1))

        @block.gpsimd
        def _(g):
            g.memset(ident[:], 0.0).then_inc(k_zero, 1)
            g.memset(ones16[:], 1.0).then_inc(k_zero, 1)
            g.wait_ge(k_zero, 2)
            g.affine_select(out=ident[:], in_=ident[:], compare_op=ALU.not_equal, fill=1.0, base=0,
                            pattern=[[-1, P]], channel_multiplier=1).then_inc(k_mask, 1)
            g.affine_select(out=before[:], in_=ones16[:], compare_op=ALU.is_gt, fill=0.0, base=0,
                            pattern=[[1, P]], channel_multiplier=-1).then_inc(k_mask, 1)
            g.memset(ctx1[:].rearrange("p (s w) -> p s w", s=S)[:, :, D:D + 1], 1.0)
            g.memset(score[:], -1e30)
            g.memset(upto[:], 1.0)
            g.memset(filler_a[:], 0.0)
            g.memset(filler_b[:, 0:D], 0.0)
            g.memset(filler_b[:, D:BW].bitcast(I32), NOTOK)
            g.memset(mhalf[:], -0.5)
            g.memset(eps_ln[:], EPS_LN)
            g.memset(cum[:, 0:E], 0.0)
            for c in range(NC):
                col = row_b[:, c * S * BW:(c + 1) * S * BW].rearrange("p (s w) -> p s w", s=S)[:, :, D:BW]
                g.iota(col.bitcast(I32), pattern=[[BATCH, S], [1, 1]], base=c * P, channel_multiplier=1)
            g.iota(rev[:], pattern=[[-1, E]], base=E, channel_multiplier=0, allow_small_or_imprecise_dtypes=True)
            g.iota(region[:], pattern=[[ROWS, E]], base=0, channel_multiplier=0, allow_small_or_imprecise_dtypes=True)
            g.iota(kcol[:], pattern=[[P, KB]], base=0, channel_multiplier=0, allow_small_or_imprecise_dtypes=True)
            g.iota(bcol[:], pattern=[[1, NB]], base=0, channel_multiplier=0, allow_small_or_imprecise_dtypes=True
                   ).then_inc(k_const, 1)
            g.wait_ge(k_const, 1)
            g.affine_select(out=upto[:], in_=upto[:], compare_op=ALU.is_ge, fill=0.0, base=0,
                            pattern=[[1, E], [-1, E]], channel_multiplier=0).then_inc(k_const, 1)

            def attn_products(c, later):
                g.wait_ge(ld_x[c] if isinstance(c, int) else ld_x[NC - 1], 16)
                bo = bias[:, 3 * D:4 * D].unsqueeze(1).to_broadcast([P, S, D])
                g.tensor_tensor(chunk_of(xb, c, CW).rearrange("p (s d) -> p s d", s=S),
                                chunk_of(x0, c, CW).rearrange("p (s d) -> p s d", s=S), bo, ALU.add).then_inc(xb_sb, 1)
                if later:
                    g.wait_ge(score_sb, 3 * c)
                for i in range(1, S):
                    g.wait_ge(qkv_sb, S * c + i + 1)
                    q = qkv_part(c, i, 0).to_broadcast([P, i + 1, D])
                    g.tensor_tensor(pq[:, PB[i] * D:(PB[i] + i + 1) * D].rearrange("p (j d) -> p j d", d=D),
                                    qkv_part(c, 0, 1, i + 1), q, ALU.mult).then_inc(pq_sb, 1)

            def rstd(n, c, mv_ready, ve_done, rs_done):
                g.wait_ge(mv_ready, S * c + S)
                at = (c * 2 + n) * S
                var = mv[:, ds(at * 2, S * 2)].rearrange("p (s w) -> p s w", w=2)[:, :, 1:2]
                g.tensor_scalar(ve[:, ds(at, S)], var, EPS_LN, None, ALU.add).then_inc(ve_done, 1)
                g.wait_ge(ve_done, c + 1)
                g.tensor_tensor(rs[:, ds(at, S)], ve[:, ds(at, S)], mhalf[:], ALU.pow).then_inc(rs_done, 1)

            def count(c):
                g.wait_ge(hot_sb, c + 1)
                for s in range(S):
                    at = c * S + s
                    if not (isinstance(at, int) and at == 0):
                        g.wait_ge(cum_sb, at)
                    g.tensor_tensor(cum[:, ds((at + 1) * E, E)], cum[:, ds(at * E, E)],
                                    hot[:, ds(at * E, E)], ALU.add).then_inc(cum_sb, 1)
                g.wait_ge(tsc_sb, c + 1)
                dst = row_a[:, ds(c * S * AW, S * AW)].rearrange("p (s w) -> p s w", s=S)[:, :, D:D + 1]
                g.tensor_scalar(dst, chunk_of(tsc, c, S).unsqueeze(2), 0.5, 0.5, ALU.mult, ALU.add).then_inc(sc_sb, 1)

            def scatter(c, rows, width, table, ready, done):
                g.wait_ge(pos_sb, c + 1)
                if ready is rowb_sb:
                    g.wait_ge(rowb_sb, c + 1)
                else:
                    g.wait_ge(x2_sb, S * c + S)
                    g.wait_ge(sc_sb, c + 1)
                for s in range(S):
                    g.indirect_dma_start(
                        out=table[:, :],
                        out_offset=bass.IndirectOffsetOnAxis(ap=pos[:, ds(c * S + s, 1)], axis=0),
                        in_=tile_of(rows, c, s, width), in_offset=None).then_inc(done, 16)

            def post(c):
                rstd(0, c, mv1_sb, ve1_sb, rs1_sb)
                rstd(1, c, mv2_sb, ve2_sb, rs2_sb)
                count(c)
                scatter(c, row_a, AW, table_a, x2_sb, scat_a)
                scatter(c, row_b, BW, table_b, rowb_sb, scat_b)

            g.wait_ge(ld_bias, 64)
            attn_products(0, False)
            for c in range(1, NC):
                attn_products(c, True)
                post(c - 1)
            post(NC - 1)

            def rstd3(b, q):
                g.wait_ge(mv3_sb, b + 1)
                g.tensor_tensor(ve3[:, q:q + 1], mv3[:, 2 * q + 1:2 * q + 2], eps_ln[:], ALU.add).then_inc(ve3_sb, 1)
                g.wait_ge(ve3_sb, b + 1)
                g.tensor_tensor(rs3[:, q:q + 1], ve3[:, q:q + 1], mhalf[:, 0:1], ALU.pow).then_inc(rs3_sb, 1)

            last_token = g.to_reg(TOK - 1)

            def send(b, q):
                g.indirect_dma_start(
                    out=out_rows, out_offset=bass.IndirectOffsetOnAxis(ap=token[:, q:q + 1], axis=0),
                    in_=fin[:, q * D:(q + 1) * D], in_offset=None,
                    bounds_check=last_token, oob_is_err=False).then_inc(out_dma[q], 16)

            rstd3(0, 0)
            with g.Fori(0, (NB - 3) // RING) as k:
                for h in range(RING):
                    rstd3(RING * k + h + 1, (h + 1) % RING)
                    send(RING * k + h, h)
            for b in range(NB - 3, NB):
                if b + 1 < NB:
                    rstd3(b + 1, (b + 1) % RING)
                g.wait_ge(fin_sb, b + 1)
                send(b, b % RING)

        @block.scalar
        def _(a):
            a.dma_start(beta[:], t["L0_attn_beta"].unsqueeze(0).to_broadcast([P, HEADS])).then_inc(ld_beta, 16)
            for n, w in enumerate(("bq", "bk", "bv", "bo")):
                a.dma_start(bias[:, n * D:(n + 1) * D], t[f"L0_attn_{w}"].unsqueeze(0).to_broadcast([P, D])).then_inc(ld_bias, 16)
            a.dma_start(ctx1[:].rearrange("p (s w) -> p s w", s=S)[:, :, 0:D],
                        t["ctx_1024"].rearrange("s l d -> l s d")).then_inc(ld_ctx, 16)
            a.dma_start(proj[:], t["L0_xattn_projection"]).then_inc(ld_proj, 16)
            a.dma_start(gate[:], t["L0_ffn_gate_w"]).then_inc(ld_gate, 16)
            a.wait_ge(ld_beta, 16)
            a.activation(qscale[:], beta[:], ACT.Exp, scale=-1.0).then_inc(qs_sb, 1)

            def copy_x0t(c):
                a.wait_ge(x0t_ps, c + 1)
                a.copy(chunk_of(x0_t, c, CW), bank[0][:]).then_inc(x0t_sb, 1)

            def exps(c):
                a.wait_ge(ssub_sb, c + 1)
                a.activation(chunk_of(prob, c, SW), chunk_of(ssub, c, SW), ACT.Exp).then_inc(exp_sb, 1)

            def copy_att(c):
                a.wait_ge(att_ps, c + 1)
                a.copy(att_t[:], bank[0][:]).then_inc(att_t_sb, 1)

            def copy_x1t(c):
                a.wait_ge(x1t_ps, c + 1)
                a.copy(x1_t[:], bank[3][:]).then_inc(x1t_sb, 1)

            def features_q(c):
                a.wait_ge(fq_ps, c + 1)
                a.activation(rf_q[:], bank[3][0:M, :], ACT.Exp, scale=INV_SQRT_D).then_inc(fq_sb, 1)

            def copy_x2t(c):
                a.wait_ge(x2t_ps, c + 1)
                a.copy(x2_t[:], bank[3][:]).then_inc(x2t_sb, 1)

            def score_tanh(c):
                a.wait_ge(ltop_sb, c + 1)
                a.activation(chunk_of(tsc, c, S), chunk_of(ltop, c, S), ACT.Tanh, scale=0.5).then_inc(tsc_sb, 1)

            def gate_tanh(c, h):
                a.wait_ge(g_ps, 2 * c + h + 1)
                a.activation(th[:, h * CW:(h + 1) * CW], bank[6 - 2 * h][:], ACT.Tanh, scale=0.5).then_inc(th_sb, 1)

            copy_x0t(0)
            a.wait_ge(fk_ps, 1)
            a.activation(rf_k[:], bank[4][0:CTX, 0:S * M], ACT.Exp, scale=INV_SQRT_D).then_inc(fk_sb, 1)
            exps(0)
            copy_att(0)
            for c in range(1, NC + 1):
                if c < NC:
                    copy_x0t(c)
                copy_x1t(c - 1)
                features_q(c - 1)
                if c < NC:
                    exps(c)
                copy_x2t(c - 1)
                score_tanh(c - 1)
                for h in range(HALVES):
                    gate_tanh(c - 1, h)
                if c < NC:
                    copy_att(c)

            def copy_xst(b, q):
                a.wait_ge(xst_ps, b + 1)
                a.copy(xs_t[:, q * D:(q + 1) * D], bank[q][:, 0:D]).then_inc(xst_sb, 1)

            def silu(b, q, r):
                a.wait_ge(gu_ps, b + 1)
                a.activation(si[:, q * I:(q + 1) * I], bank[2 + q][:, 0:I], ACT.Silu,
                             scale=xs[:, r * AW + D:r * AW + D + 1]).then_inc(si_sb, 1)

            def copy_act(b, q):
                a.wait_ge(act_ps, b + 1)
                a.copy(ac_t[:, q * I:(q + 1) * I], bank[4 + q][:, 0:I]).then_inc(act_sb, 1)

            copy_xst(0, 0)
            copy_xst(1, 1)
            silu(0, 0, 0)
            with a.Fori(0, (NB - 3) // RING) as k:
                for h in range(RING):
                    b = RING * k + h
                    copy_xst(b + 2, h % 2)
                    copy_act(b, h % 2)
                    silu(b + 1, (h + 1) % 2, (h + 1) % RING)
            for b in range(NB - 3, NB):
                if b + 2 < NB:
                    copy_xst(b + 2, b % 2)
                copy_act(b, b % 2)
                if b + 1 < NB:
                    silu(b + 1, (b + 1) % 2, (b + 1) % RING)

        @block.vector
        def _(v):
            v.wait_ge(k_const, 1)
            v.wait_ge(w_ps, 1)
            v.wait_ge(qs_sb, 1)
            heads = lambda ap: ap.rearrange("p (h d) -> p h d", h=HEADS)
            scale_b = qscale[:].unsqueeze(2).to_broadcast([P, HEADS, DH])
            v.scalar_tensor_tensor(heads(w_t[:, 0:D]), heads(bank[0][:, 0:D]), INV_SQRT_DH, scale_b,
                                   ALU.mult, ALU.mult).then_inc(w_sb, 1)
            v.tensor_copy(w_t[:, D:4 * D], bank[0][:, D:4 * D]).then_inc(w_sb, 1)
            v.wait_ge(ld_bias, 64)
            v.scalar_tensor_tensor(heads(bias[:, 0:D]), heads(bias[:, 0:D]), INV_SQRT_DH, scale_b,
                                   ALU.mult, ALU.mult).then_inc(bq_sb, 1)

            def project_bias(c):
                for s in range(S):
                    v.wait_ge(qkv_ps, S * c + s + 1)
                    v.tensor_tensor(qkv[:, ds((c * S + s) * 3 * D, 3 * D)], bank[1 + s % 2][:, 0:3 * D],
                                    bias[:, 0:3 * D], ALU.add).then_inc(qkv_sb, 1)

            def scores(c):
                for i in range(1, S):
                    v.wait_ge(pq_sb, 3 * c + i)
                    at = c * SW + (i - 1) * S * HEADS
                    v.tensor_reduce(score[:, ds(at, (i + 1) * HEADS)],
                                    pq[:, PB[i] * D:(PB[i] + i + 1) * D].rearrange("p (g d) -> p g d", d=DH),
                                    X, ALU.add).then_inc(score_sb, 1)

            def by_query(ap):
                return ap.rearrange("p (i j h) -> p i h j", i=S - 1, j=S)

            SQ = (S - 1) * HEADS

            def over_keys(ap):
                return ap.rearrange("p (i h) -> p i h", i=S - 1).unsqueeze(3).to_broadcast([P, S - 1, HEADS, S])

            def softmax_max(c):
                v.wait_ge(score_sb, 3 * c + 3)
                v.tensor_reduce(chunk_of(smax, c, SQ), by_query(chunk_of(score, c, SW)), X, ALU.max).then_inc(smax_sb, 1)

            def softmax_sub(c):
                v.wait_ge(smax_sb, c + 1)
                v.tensor_tensor(by_query(chunk_of(ssub, c, SW)), by_query(chunk_of(score, c, SW)),
                                over_keys(chunk_of(smax, c, SQ)), ALU.subtract).then_inc(ssub_sb, 1)

            def softmax_sum(c):
                v.wait_ge(exp_sb, c + 1)
                v.tensor_reduce(chunk_of(ssum, c, SQ), by_query(chunk_of(prob, c, SW)), X, ALU.add).then_inc(ssum_sb, 1)
                v.wait_ge(ssum_sb, c + 1)
                v.reciprocal(chunk_of(srec, c, SQ), chunk_of(ssum, c, SQ)).then_inc(srec_sb, 1)
                v.wait_ge(srec_sb, c + 1)
                v.tensor_tensor(by_query(chunk_of(prob, c, SW)), by_query(chunk_of(prob, c, SW)),
                                over_keys(chunk_of(srec, c, SQ)), ALU.mult).then_inc(prob_sb, 1)

            def attend(c):
                v.wait_ge(prob_sb, c + 1)
                if not (isinstance(c, int) and c == 0):
                    v.wait_ge(att_sb, 3 * c)
                for i in range(1, S):
                    n = (i + 1) * HEADS
                    p = prob[:, ds(c * SW + (i - 1) * S * HEADS, n)].rearrange("p (j h) -> p j h", h=HEADS)
                    v.tensor_tensor(
                        pv[:, PB[i] * D:(PB[i] + i + 1) * D].rearrange("p (j h d) -> p j h d", h=HEADS, d=DH),
                        qkv_part(c, 0, 2, i + 1).rearrange("p j (h d) -> p j h d", d=DH),
                        p.unsqueeze(3).to_broadcast([P, i + 1, HEADS, DH]), ALU.mult).then_inc(pv_sb, 1)
                for i in range(1, S):
                    v.wait_ge(pv_sb, 3 * c + i)
                    v.tensor_reduce(att[:, ds((c * (S - 1) + i - 1) * D, D)],
                                    pv[:, PB[i] * D:(PB[i] + i + 1) * D].rearrange("p (j w) -> p w j", w=D),
                                    X, ALU.add).then_inc(att_sb, 1)

            def stats(n, c, src, ready, st_done, mv_done):
                for s in range(S):
                    if s == 0 or ready is r2_sb:
                        v.wait_ge(ready, S * c + s + 1 if ready is r2_sb else c + 1)
                    v.bn_stats(st[:, ds(((c * 2 + n) * S + s) * 6, 6)], src[:, s * D:(s + 1) * D]).then_inc(st_done, 1)
                for s in range(S):
                    v.wait_ge(st_done, S * c + s + 1)
                    v.bn_aggr(mv[:, ds(((c * 2 + n) * S + s) * 2, 2)],
                              st[:, ds(((c * 2 + n) * S + s) * 6, 6)]).then_inc(mv_done, 1)

            def normed(n, c, src, dst, width, row, rs_ready, done):
                v.wait_ge(rs_ready, c + 1)
                for s in range(S):
                    at = (c * 2 + n) * S + s
                    v.tensor_scalar(dst[:, ds((c * S + s) * row, width)], src[:, s * D:(s + 1) * D],
                                    mv[:, ds(at * 2, 1)], rs[:, ds(at, 1)], ALU.subtract, ALU.mult).then_inc(done, 1)

            def residual1(c):
                v.wait_ge(ao_ps, c + 1)
                v.wait_ge(xb_sb, c + 1)
                if not (isinstance(c, int) and c == 0):
                    v.wait_ge(x1_sb, S * c)
                v.tensor_tensor(r1[:], bank[1][:], chunk_of(xb, c, CW), ALU.add).then_inc(r1_sb, 1)

            def residual2(c):
                v.wait_ge(xo_ps, c + 1)
                both = [bank[4], bank[5]]
                for n in range(2):
                    z = both[n][:].rearrange("p (s w) -> p s w", s=2)[:, :, D:D + 1]
                    v.tensor_scalar(den[:, ds(c * S + 2 * n, 2)].unsqueeze(2), z, EPS_X, None, ALU.add).then_inc(den_sb, 1)
                v.wait_ge(den_sb, 2 * c + 2)
                v.reciprocal(chunk_of(rden, c, S), chunk_of(den, c, S)).then_inc(rden_sb, 1)
                v.wait_ge(rden_sb, c + 1)
                if not (isinstance(c, int) and c == 0):
                    v.wait_ge(x2_sb, S * c)
                for s in range(S):
                    v.scalar_tensor_tensor(r2[:, s * D:(s + 1) * D], both[s // 2][:, (s % 2) * 256:(s % 2) * 256 + D],
                                           rden[:, ds(c * S + s, 1)], tile_of(x1, c, s),
                                           ALU.mult, ALU.add).then_inc(r2_sb, 1)

            def route(c):
                by_tile = lambda ap: ap.rearrange("p (s e) -> p s e", s=S)
                over_e = lambda ap: ap.unsqueeze(2).to_broadcast([P, S, E])
                lg = by_tile(bank[3][:, 0:S * E])
                W = S * E
                v.wait_ge(lg_ps, c + 1)
                v.tensor_reduce(chunk_of(ltop, c, S), lg, X, ALU.max).then_inc(ltop_sb, 1)
                v.wait_ge(ltop_sb, c + 1)
                v.tensor_tensor(by_tile(chunk_of(leq, c, W)), lg, over_e(chunk_of(ltop, c, S)), ALU.is_equal).then_inc(leq_sb, 1)
                v.wait_ge(leq_sb, c + 1)
                v.tensor_tensor(by_tile(chunk_of(lcand, c, W)), by_tile(chunk_of(leq, c, W)),
                                rev[:].unsqueeze(1).to_broadcast([P, S, E]), ALU.mult).then_inc(lcand_sb, 1)
                v.wait_ge(lcand_sb, c + 1)
                v.tensor_reduce(chunk_of(lfirst, c, S), by_tile(chunk_of(lcand, c, W)), X, ALU.max).then_inc(lfirst_sb, 1)
                v.wait_ge(lfirst_sb, c + 1)
                v.tensor_tensor(by_tile(chunk_of(hot, c, W)), by_tile(chunk_of(lcand, c, W)),
                                over_e(chunk_of(lfirst, c, S)), ALU.is_equal).then_inc(hot_sb, 1)

            def place(c):
                by_tile = lambda ap: ap.rearrange("p (s e) -> p s e", s=S)
                W = S * E
                v.wait_ge(rank_ps, c + 1)
                v.tensor_tensor(by_tile(chunk_of(rk, c, W)), by_tile(bank[3][:, 0:W]),
                                region[:].unsqueeze(1).to_broadcast([P, S, E]), ALU.add).then_inc(rk_sb, 1)
                v.wait_ge(rk_sb, c + 1)
                v.tensor_tensor(chunk_of(rkh, c, W), chunk_of(rk, c, W), chunk_of(hot, c, W), ALU.mult).then_inc(rkh_sb, 1)
                v.wait_ge(rkh_sb, c + 1)
                with nc.allow_low_precision(reason="row numbers are whole and under 2**24: exact in float32"):
                    v.tensor_reduce(chunk_of(pos, c, S), by_tile(chunk_of(rkh, c, W)), X, ALU.add).then_inc(pos_sb, 1)

            def shared_hidden(c, h):
                v.wait_ge(th_sb, 2 * c + h + 1)
                if not (isinstance(c, int) and c == 0):
                    v.wait_ge(hid_sb, 2 * c + h)
                v.scalar_tensor_tensor(hg[:, h * CW:(h + 1) * CW], th[:, h * CW:(h + 1) * CW], 1.0,
                                       bank[6 - 2 * h][:], ALU.add, ALU.mult).then_inc(hg_sb, 1)
                v.wait_ge(hg_sb, 2 * c + h + 1)
                v.tensor_tensor(hid[:, h * CW:(h + 1) * CW], hg[:, h * CW:(h + 1) * CW],
                                bank[7 - 2 * h][:], ALU.mult).then_inc(hid_sb, 1)

            def shared_out(c):
                v.wait_ge(sy_ps, c + 1)
                x2 = row_a[:, ds(c * S * AW, S * AW)].rearrange("p (s w) -> p s w", s=S)[:, :, 0:D]
                v.tensor_tensor(row_b[:, ds(c * S * BW, S * BW)].rearrange("p (s w) -> p s w", s=S)[:, :, 0:D],
                                bank[6][:].rearrange("p (s d) -> p s d", s=S), x2, ALU.add).then_inc(rowb_sb, 1)

            v.wait_ge(bq_sb, 1)
            project_bias(0)
            v.wait_ge(c_ps, 1)
            v.tensor_copy(proj_t[:], bank[3][:, 0:M]).then_inc(c_sb, 1)
            v.tensor_copy(ctx_t[:], bank[3][:, M:M + S * CTX]).then_inc(c_sb, 1)
            scores(0)
            softmax_max(0)
            v.wait_ge(kv_ps, 1)
            for n in range(2):
                v.tensor_scalar(kvz[:, 2 * n * (D + 1):2 * (n + 1) * (D + 1)].rearrange("p (s w) -> p s w", s=2),
                                bank[4 + n][0:M, :].rearrange("p (s w) -> p s w", s=2)[:, :, 0:D + 1],
                                1.0 / math.sqrt(M), None, ALU.mult).then_inc(kv_sb, 1)
            softmax_sub(0)
            v.wait_ge(ld_sh, 48)
            v.tensor_scalar(sh_dn[:], sh_dn[:], 0.5, None, ALU.mult).then_inc(kv_sb, 1)
            softmax_sum(0)
            attend(0)
            for c in range(1, NC + 1):
                residual1(c - 1)
                if c < NC:
                    project_bias(c)
                stats(0, c - 1, r1, r1_sb, st1_sb, mv1_sb)
                if c < NC:
                    scores(c)
                normed(0, c - 1, r1, x1, D, D, rs1_sb, x1_sb)
                if c < NC:
                    softmax_max(c)
                    softmax_sub(c)
                residual2(c - 1)
                stats(1, c - 1, r2, r2_sb, st2_sb, mv2_sb)
                if c < NC:
                    softmax_sum(c)
                normed(1, c - 1, r2, row_a, D, AW, rs2_sb, x2_sb)
                if c < NC:
                    attend(c)
                route(c - 1)
                if c == NC:
                    place(c - 1)
                for h in range(HALVES):
                    shared_hidden(c - 1, h)
                if c < NC:
                    place(c - 1)
                    shared_out(c - 1)

            step = [0]

            def tabled(ins):
                step[0] += 1
                ins.then_inc(tab, 1)
                v.wait_ge(tab, step[0])

            v.wait_ge(cnt_ps, 1)
            v.wait_ge(k_const, 2)
            tabled(v.tensor_copy(cnt[:], bank[3][0:1, 0:E]))
            g3 = gtk[:].rearrange("p (e k) -> p e k", e=E)
            tabled(v.tensor_tensor(g3, cnt[:].unsqueeze(2).to_broadcast([1, E, KB]),
                                   kcol[:].unsqueeze(1).to_broadcast([1, E, KB]), ALU.is_gt))
            tabled(v.tensor_reduce(nblk[:], g3, X, ALU.add))
            m3 = nmask[:].rearrange("p (e f) -> p e f", e=E)
            tabled(v.tensor_tensor(m3, upto[:].rearrange("p (e f) -> p e f", e=E),
                                   nblk[:].unsqueeze(1).to_broadcast([1, E, E]), ALU.mult))
            tabled(v.tensor_reduce(cblk[:], m3, X, ALU.add))
            tabled(v.tensor_scalar(dstep[:], nblk[:], -float(P), float(ROWS), ALU.mult, ALU.add))
            ge3 = ge[:].rearrange("p (b e) -> p b e", e=E)
            ged3 = ged[:].rearrange("p (b e) -> p b e", e=E)
            tabled(v.tensor_tensor(ge3, bcol[:].unsqueeze(2).to_broadcast([1, NB, E]),
                                   cblk[:].unsqueeze(1).to_broadcast([1, NB, E]), ALU.is_ge))
            tabled(v.tensor_tensor(ged3, ge3, dstep[:].unsqueeze(1).to_broadcast([1, NB, E]), ALU.mult))
            tabled(v.tensor_reduce(rsum[:], ged3, X, ALU.add))
            tabled(v.scalar_tensor_tensor(radd[:], bcol[:], float(P), rsum[:], ALU.mult, ALU.add))
            tabled(v.tensor_scalar(blk_row[:], radd[:], float(FILLER), None, ALU.min))
            tabled(v.tensor_tensor(tail_row[:], cnt[:], region[0:1, :], ALU.add))
            v.tensor_reduce(esum[:], ge3, X, ALU.add).then_inc(tab, 1)
            v.wait_ge(tab, TAB)
            v.tensor_scalar(blk_e[:], esum[:], float(E - 1), None, ALU.min).then_inc(tab, 1)
            shared_out(NC - 1)

            def gated(b, q, r):
                v.wait_ge(si_sb, b + 1)
                v.wait_ge(ld_xs[r], 16)
                v.scalar_tensor_tensor(ac[:, q * I:(q + 1) * I], bank[2 + q][:, I:2 * I],
                                       xs[:, r * AW + D:r * AW + D + 1], si[:, q * I:(q + 1) * I],
                                       ALU.mult, ALU.mult).then_inc(ac_sb, 1)

            def residual3(b, q, r, nth):
                v.wait_ge(y_ps, b + 1)
                v.wait_ge(ld_bs[r], 16 * nth + 16)
                if not (isinstance(nth, int) and nth == 0):
                    v.wait_ge(out_dma[r], 16 * nth)
                v.tensor_copy(token[:, r:r + 1], bs[:, r * BW + D:(r + 1) * BW].bitcast(I32))
                v.tensor_tensor(r3[:, r * D:(r + 1) * D], bank[6 + q][:, 0:D], bs[:, r * BW:r * BW + D],
                                ALU.add).then_inc(r3_sb, 1)

            def stats3(b, r):
                v.wait_ge(r3_sb, b + 1)
                v.bn_stats(st3[:, r * 6:(r + 1) * 6], r3[:, r * D:(r + 1) * D]).then_inc(st3_sb, 1)

            def aggr3(b, r):
                v.bn_aggr(mv3[:, 2 * r:2 * r + 2], st3[:, r * 6:(r + 1) * 6]).then_inc(mv3_sb, 1)

            def normed3(b, r):
                v.wait_ge(rs3_sb, b + 1)
                v.tensor_scalar(fin[:, r * D:(r + 1) * D], r3[:, r * D:(r + 1) * D], mv3[:, 2 * r:2 * r + 1],
                                rs3[:, r:r + 1], ALU.subtract, ALU.mult).then_inc(fin_sb, 1)

            gated(0, 0, 0)
            gated(1, 1, 1)
            LOOPS = (NB - 3) // RING
            def step3(b, h, nth, gate_next=True, norm_last=True):
                residual3(b, h % 2, h % RING, nth)
                if gate_next:
                    gated(b + 2, h % 2, (h + 2) % RING)
                stats3(b, h % RING)
                v.wait_ge(st3_sb, b + 1)
                if norm_last:
                    normed3(b - 1, (h + 3) % RING)
                aggr3(b, h % RING)

            step3(0, 0, 0, norm_last=False)
            for h in range(1, RING):
                step3(h, h, 0)
            with v.Fori(0, LOOPS - 1) as k:
                for h in range(RING):
                    step3(RING * k + RING + h, h, k + 1)
            for b in range(RING * LOOPS, NB):
                step3(b, b % RING, b // RING, gate_next=b + 2 < NB)
            normed3(NB - 1, (NB - 1) % RING)

        @block.tensor
        def _(pe):
            pe.wait_ge(k_mask, 2)
            pe.wait_ge(ld_w, 64)
            for n in range(4):
                last = pe.transpose(bank[0][:, n * P:(n + 1) * P], w_nat[:, n * P:(n + 1) * P], ident[:])
            last.then_inc(w_ps, 1)

            def x0_transposes(c):
                if isinstance(c, int):
                    pe.wait_ge(ld_x[c], 16)
                if isinstance(c, int) and c == 0:
                    pe.wait_ge(w_sb, 2)
                else:
                    pe.wait_ge(att_t_sb, c)
                for s in range(S):
                    last = pe.transpose(bank[0][:, s * D:(s + 1) * D], tile_of(x0, c, s), ident[:])
                last.then_inc(x0t_ps, 1)

            def project(c):
                pe.wait_ge(x0t_sb, c + 1)
                for s in range(S):
                    if not (isinstance(c, int) and c == 0):
                        if s == 0:
                            pe.wait_ge(r1_sb, c)
                        if s == 1:
                            pe.wait_ge(qkv_sb, S * c)
                    if s >= 2:
                        pe.wait_ge(qkv_sb, S * c + s - 1)
                    pe.matmul(bank[1 + s % 2][:, 0:3 * D], tile_of(x0_t, c, s), w_t[:, 0:3 * D],
                              start=True, stop=True).then_inc(qkv_ps, 1)

            def att_transposes(c):
                pe.wait_ge(att_sb, 3 * c + 3)
                pe.wait_ge(x0t_sb, c + 1)
                pe.wait_ge(qkv_sb, S * c + 1)
                v0 = qkv[:, ds(c * S * 3 * D + 2 * D, D)]
                pe.transpose(bank[0][:, 0:D], v0, ident[:])
                for i in range(1, S):
                    last = pe.transpose(bank[0][:, i * D:(i + 1) * D], att[:, ds((c * (S - 1) + i - 1) * D, D)], ident[:])
                last.then_inc(att_ps, 1)

            def att_out(c):
                pe.wait_ge(att_t_sb, c + 1)
                pe.wait_ge(qkv_sb, S * c + S)
                for s in range(S):
                    last = pe.matmul(bank[1][:, s * D:(s + 1) * D], att_t[:, s * D:(s + 1) * D], w_t[:, 3 * D:4 * D],
                                     start=True, stop=True)
                last.then_inc(ao_ps, 1)

            def x1_transposes(c):
                pe.wait_ge(x1_sb, S * c + S)
                if isinstance(c, int) and c == 0:
                    pe.wait_ge(c_sb, 2)
                else:
                    pe.wait_ge(pos_sb, c)
                for s in range(S):
                    last = pe.transpose(bank[3][:, s * D:(s + 1) * D], tile_of(x1, c, s), ident[:])
                last.then_inc(x1t_ps, 1)

            def features(c):
                pe.wait_ge(x1t_sb, c + 1)
                pe.matmul(bank[3][0:M, :], proj_t[:], x1_t[:], start=True, stop=True).then_inc(fq_ps, 1)

            def cross_out(c):
                pe.wait_ge(fq_sb, c + 1)
                if isinstance(c, int) and c == 0:
                    pe.wait_ge(kv_sb, 3)
                else:
                    pe.wait_ge(hid_sb, 2 * c)
                for s in range(S):
                    last = pe.matmul(bank[4 + s // 2][:, (s % 2) * 256:(s % 2) * 256 + D + 1],
                                     rf_q[:, s * D:(s + 1) * D], kvz[:, s * (D + 1):(s + 1) * (D + 1)],
                                     start=True, stop=True)
                last.then_inc(xo_ps, 1)

            def x2_transposes(c):
                pe.wait_ge(x2_sb, S * c + S)
                pe.wait_ge(fq_sb, c + 1)
                for s in range(S):
                    last = pe.transpose(bank[3][:, s * D:(s + 1) * D], row_a[:, ds((c * S + s) * AW, D)], ident[:])
                last.then_inc(x2t_ps, 1)

            def logits(c):
                pe.wait_ge(x2t_sb, c + 1)
                for s in range(S):
                    last = pe.matmul(bank[3][:, s * E:(s + 1) * E], x2_t[:, s * D:(s + 1) * D], gate[:],
                                     start=True, stop=True)
                last.then_inc(lg_ps, 1)

            def rank(c):
                pe.wait_ge(hot_sb, c + 1)
                pe.wait_ge(cum_sb, S * c + S)
                W = S * E
                pe.matmul(bank[3][:, 0:W], before[:], chunk_of(hot, c, W), start=True, stop=False)
                pe.matmul(bank[3][:, 0:W], ones16[:], chunk_of(cum, c, W), start=False, stop=True).then_inc(rank_ps, 1)

            def shared_up(c):
                for h in range(HALVES):
                    if h == 0:
                        if not (isinstance(c, int) and c == 0):
                            pe.wait_ge(rowb_sb, c)
                    else:
                        pe.wait_ge(r2_sb, S * c + S)
                    pe.matmul(bank[7 - 2 * h][:], sh_gu[:, I + h * P:I + (h + 1) * P], x2_t[:], start=True, stop=True)
                    pe.matmul(bank[6 - 2 * h][:], sh_gu[:, h * P:(h + 1) * P], x2_t[:], start=True, stop=True).then_inc(g_ps, 1)

            def shared_down(c):
                pe.wait_ge(hid_sb, 2 * c + 2)
                for s in range(S):
                    for h in range(HALVES):
                        last = pe.matmul(bank[6][:, s * D:(s + 1) * D], hid[:, h * CW + s * D:h * CW + (s + 1) * D],
                                         sh_dn[:, h * D:(h + 1) * D], start=h == 0, stop=h == HALVES - 1)
                last.then_inc(sy_ps, 1)

            x0_transposes(0)
            project(0)
            pe.wait_ge(ld_ctx, 16)
            pe.wait_ge(ld_proj, 16)
            pe.wait_ge(k_const, 1)
            pe.transpose(bank[3][:, 0:M], proj[:], ident[0:M, 0:M])
            c3 = ctx1[:].rearrange("p (s w) -> p s w", s=S)
            for s in range(S):
                last = pe.transpose(bank[3][:, M + s * CTX:M + (s + 1) * CTX], c3[:, s, 0:D], ident[0:CTX, 0:CTX])
            last.then_inc(c_ps, 1)
            pe.wait_ge(c_sb, 2)
            for s in range(S):
                last = pe.matmul(bank[4][0:CTX, s * M:(s + 1) * M], ctx_t[:, s * CTX:(s + 1) * CTX], proj_t[:],
                                 start=True, stop=True)
            last.then_inc(fk_ps, 1)
            pe.wait_ge(fk_sb, 1)
            for s in range(S):
                last = pe.matmul(bank[4 + s // 2][0:M, (s % 2) * 256:(s % 2) * 256 + D + 1], rf_k[:, s * M:(s + 1) * M],
                                 ctx1[:, s * (D + 1):(s + 1) * (D + 1)], start=True, stop=True)
            last.then_inc(kv_ps, 1)
            att_transposes(0)
            att_out(0)
            pe.wait_ge(ld_gate, 16)
            pe.wait_ge(ld_sh, 48)
            for c in range(1, NC + 1):
                if c < NC:
                    x0_transposes(c)
                    project(c)
                x1_transposes(c - 1)
                features(c - 1)
                cross_out(c - 1)
                x2_transposes(c - 1)
                logits(c - 1)
                if c == NC:
                    rank(c - 1)
                shared_up(c - 1)
                if c < NC:
                    att_transposes(c)
                    rank(c - 1)
                    att_out(c)
                if c == NC:
                    pe.wait_ge(pos_sb, NC)
                    pe.matmul(bank[3][:, 0:E], ones16[:], cum[:, NC * S * E:(NC * S + 1) * E], start=True, stop=True
                              ).then_inc(cnt_ps, 1)
                shared_down(c - 1)

            def turn(b, q, r, nth, reuse=True):
                pe.wait_ge(ld_xs[r], 16 * nth + 16)
                if reuse:
                    pe.wait_ge(xst_sb, b - 1)
                pe.transpose(bank[q][:, 0:D], xs[:, r * AW:r * AW + D], ident[:]).then_inc(xst_ps, 1)

            def up(b, q, reuse=True):
                ex = pe.value_load(blk_e[0:1, ds(b, 1)], min_val=0, max_val=E - 1)
                pe.wait_ge(xst_sb, b + 1)
                if reuse:
                    pe.wait_ge(ac_sb, b - 1)
                pe.matmul(bank[2 + q][:], xs_t[:, q * D:(q + 1) * D], rt_gu[:, ds(ex * (2 * I), 2 * I)],
                          start=True, stop=True).then_inc(gu_ps, 1)

            def turn_hidden(b, q, reuse=True):
                pe.wait_ge(ac_sb, b + 1)
                if reuse:
                    pe.wait_ge(act_sb, b - 1)
                for h in range(HALVES):
                    last = pe.transpose(bank[4 + q][:, h * P:(h + 1) * P], ac[:, q * I + h * P:q * I + (h + 1) * P], ident[:])
                last.then_inc(act_ps, 1)

            def down(b, q, reuse=True):
                ex = pe.value_load(blk_e[0:1, ds(b, 1)], min_val=0, max_val=E - 1)
                pe.wait_ge(act_sb, b + 1)
                if reuse:
                    pe.wait_ge(r3_sb, b - 1)
                for h in range(HALVES):
                    last = pe.matmul(bank[6 + q][:, 0:D], ac_t[:, q * I + h * P:q * I + (h + 1) * P],
                                     rt_dn[:, ds(ex * (HALVES * D) + h * D, D)], start=h == 0, stop=h == HALVES - 1)
                last.then_inc(y_ps, 1)

            pe.wait_ge(ld_rt, 48)
            pe.wait_ge(tab, TAB + 1)
            pe.wait_ge(rowb_sb, NC)
            turn(0, 0, 0, 0, False)
            turn(1, 1, 1, 0, False)
            up(0, 0, False)
            turn(2, 0, 2, 0)
            up(1, 1, False)
            turn_hidden(0, 0, False)
            def step(b, h, nth, first=False):
                turn(b + 1, (h + 1) % 2, (h + 3) % RING, nth)
                up(b, h % 2)
                turn_hidden(b - 1, (h + 1) % 2, not (first and h == 0))
                down(b - 2, h % 2, not (first and h < 2))

            for h in range(RING):
                step(h + 2, h, 1 if h else 0, first=True)
            with pe.Fori(0, (NB - 3) // RING - 1) as k:
                for h in range(RING):
                    step(RING * k + (RING + 2 + h), h, k + (2 if h else 1))
            up(NB - 1, (NB - 1) % 2)
            turn_hidden(NB - 2, (NB - 2) % 2)
            down(NB - 3, (NB - 3) % 2)
            turn_hidden(NB - 1, (NB - 1) % 2)
            down(NB - 2, (NB - 2) % 2)
            down(NB - 1, (NB - 1) % 2)


_INS = ["x", "ctx_1024", "L0_attn_Wq", "L0_attn_bq", "L0_attn_Wk", "L0_attn_bk", "L0_attn_Wv", "L0_attn_bv",
        "L0_attn_Wo", "L0_attn_bo", "L0_attn_beta", "L0_xattn_projection", "L0_ffn_gate_w", "L0_ffn_sh_gate",
        "L0_ffn_sh_up", "L0_ffn_sh_down", "L0_ffn_rt_gate", "L0_ffn_rt_up", "L0_ffn_rt_down"]


def kernel(**inputs):
    import concourse.bacc as bacc
    from concourse.bass_utils import run_bass_kernel_spmd

    nc = bacc.Bacc("TRN2", target_bir_lowering=False, num_devices=1)
    arrays, t = {}, {}
    for name in _INS:
        a = np.ascontiguousarray(inputs[name])
        arrays[f"in_{name}"] = a
        t[name] = nc.dram_tensor(f"in_{name}", a.shape, mybir.dt.from_np(a.dtype), kind="ExternalInput").ap()
    t["out"] = nc.dram_tensor("out_x", inputs["x"].shape, mybir.dt.float32, kind="ExternalOutput").ap()
    build_decoder(nc, t)
    r = run_bass_kernel_spmd(nc, [arrays], core_ids=[0])
    return r.results[0]["out_x"]
```

```python
import math
from contextlib import ExitStack

import numpy as np

import concourse.bass as bass
from concourse import mybir


def build_decoder(nc, t):
    F32 = mybir.dt.float32
    BF16 = mybir.dt.bfloat16
    I32 = mybir.dt.int32
    ALU = mybir.AluOpType
    ACT = mybir.ActivationFunctionType
    X = mybir.AxisListType.X
    ds = bass.ds

    P = 128
    S, BATCH, D = t["x"].shape
    NC = BATCH // P
    TOK = S * BATCH
    HEADS, DH = 16, D // 16
    CTX = t["ctx_1024"].shape[1]
    M = t["L0_xattn_projection"].shape[0]
    E, _, I = t["L0_ffn_rt_gate"].shape
    HALVES = I // P
    PAIRS = S * (S + 1) // 2 - 1
    PB = [0, 0, 2, 5]
    EPS_LN, EPS_X = 1e-5, 1e-6
    INV_SQRT_D = 1.0 / math.sqrt(D)
    INV_SQRT_DH = 1.0 / math.sqrt(DH)
    NB = TOK // P + E - 1
    ROWS = TOK + P
    FILLER = E * ROWS
    AT_SCORE, AT_BASE, AT_TOKEN = D, D + 1, 2 * D + 1
    RW = 2 * D + 2
    NOTOK = 1 << 20
    KB = TOK // P
    RING = 6
    NBP = -(-NB // RING) * RING

    x_in = t["x"].rearrange("s (c p) d -> c p s d", p=P)
    out_rows = t["out"].rearrange("s b d -> (s b) d")

    ctx = ExitStack()
    with ctx:
        def sb(name, shape, dt=F32):
            return ctx.enter_context(nc.sbuf_tensor(name, shape, dt))

        def sem(name):
            return ctx.enter_context(nc.semaphore(name))

        table = nc.dram_tensor("slot_table", (FILLER + P, RW), F32, kind="Internal").ap()

        ident = sb("ident", [P, P])
        before = sb("before", [P, P], BF16)
        ones16 = sb("ones16", [P, P], BF16)
        rev = sb("rev", [P, E])
        region = sb("region", [P, E])
        kcol = sb("kcol", [1, KB])
        bcol = sb("bcol", [1, NBP])
        upto = sb("upto", [1, E * E])
        spread = sb("spread", [65, P], BF16)
        bias3 = sb("bias3", [65, 4 * P], BF16)
        brest = sb("brest", [65, 4 * P])
        mhalf = sb("mhalf", [P, S])
        filler = sb("filler", [P, RW])
        w_nat = sb("w_nat", [P, 4 * P])
        w_t = sb("w_t", [P, 4 * P])
        bias = sb("bias", [P, 4 * P])
        beta = sb("beta", [P, HEADS])
        silu_warm = sb("silu_warm", [1, 1])
        qscale = sb("qscale", [P, HEADS])
        proj = sb("proj", [M, D])
        proj_t = sb("proj_t", [D, M])
        ctx1 = sb("ctx1", [CTX, S * (D + 1)])
        ctx_t = sb("ctx_t", [D, S * CTX])
        rf_k = sb("rf_k", [CTX, S * M])
        kvz = sb("kvz", [M, S * (D + 1)])
        gate = sb("gate", [D, E])
        sh_gu = sb("sh_gu", [D, 2 * I])
        sh_dn = sb("sh_dn", [P, HALVES * D])
        rt_gu = sb("rt_gu", [D, E * 2 * I])
        rt_dn = sb("rt_dn", [P, E * HALVES * D])

        CW = S * D
        x0 = sb("x0", [P, NC * CW])
        x0_t = sb("x0_t", [P, NC * CW])
        qkv = sb("qkv", [P, NC * S * 3 * D])
        pq = sb("pq", [P, PAIRS * D])
        SW = (S - 1) * S * HEADS
        score = sb("score", [P, NC * SW])
        smax = sb("smax", [P, NC * (S - 1) * HEADS])
        ssub = sb("ssub", [P, NC * SW])
        prob = sb("prob", [P, NC * SW])
        ssum = sb("ssum", [P, NC * (S - 1) * HEADS])
        srec = sb("srec", [P, NC * (S - 1) * HEADS])
        pv = sb("pv", [P, PAIRS * D])
        att_t = sb("att_t", [P, CW])
        r2 = sb("r2", [P, CW])
        st = sb("st", [P, NC * 2 * S * 6])
        mv = sb("mv", [P, NC * 2 * S * 2])
        ve = sb("ve", [P, NC * 2 * S])
        rs = sb("rs", [P, NC * 2 * S])
        x1 = sb("x1", [P, NC * CW])
        x1_t = sb("x1_t", [P, CW])
        rf_q = sb("rf_q", [M, CW])
        den = sb("den", [P, NC * S])
        rden = sb("rden", [P, NC * S])
        rows = sb("rows", [P, NC * S * RW])
        x2_t = sb("x2_t", [P, NC * CW])
        sg = sb("sg", [P, HALVES * CW])
        hid = sb("hid", [P, 2 * HALVES * CW])
        ltop = sb("ltop", [P, NC * S])
        leq = sb("leq", [P, NC * S * E])
        lcand = sb("lcand", [P, NC * S * E])
        lfirst = sb("lfirst", [P, NC * S])
        hot = sb("hot", [P, NC * S * E], BF16)
        cum = sb("cum", [P, (NC * S + 1) * E], BF16)
        tsc = sb("tsc", [P, NC * S])
        rk = sb("rk", [P, NC * S * E])
        rkh = sb("rkh", [P, NC * S * E])
        pos = sb("pos", [P, NC * S], I32)

        cnt = sb("cnt", [1, E])
        gtk = sb("gtk", [1, E * KB])
        nblk = sb("nblk", [1, E])
        nmask = sb("nmask", [1, E * E])
        cblk = sb("cblk", [1, E])
        dstep = sb("dstep", [1, E])
        ge = sb("ge", [1, NBP * E])
        ged = sb("ged", [1, NBP * E])
        esum = sb("esum", [1, NBP])
        rsum = sb("rsum", [1, NBP])
        radd = sb("radd", [1, NBP])
        blk_e = sb("blk_e", [1, NBP], I32)
        blk_row = sb("blk_row", [1, NBP], I32)
        tail_row = sb("tail_row", [1, E], I32)

        slots = sb("slots", [P, RING * RW])
        token = sb("token", [P, RING], I32)
        xs_t = sb("xs_t", [P, 2 * D])
        si = sb("si", [P, 2 * I])
        ac = sb("ac", [P, 2 * I])
        ac_t = sb("ac_t", [P, 2 * I])
        r3 = sb("r3", [P, RING * D])
        st3 = sb("st3", [P, RING * 6])
        mv3 = sb("mv3", [P, RING * 2])
        ve3 = sb("ve3", [P, RING])
        rs3 = sb("rs3", [P, RING])
        fin = sb("fin", [P, RING * D])

        bank = [ctx.enter_context(nc.psum_tensor(f"bank{i}", [P, 512], F32)) for i in range(8)]

        ld_w, ld_bias, ld_beta, ld_ctx, ld_proj, ld_gate = map(
            sem, ["ld_w", "ld_bias", "ld_beta", "ld_ctx", "ld_proj", "ld_gate"])
        ld_x = [sem(f"ld_x{c}") for c in range(NC)]
        ld_sh, ld_rt = sem("ld_sh"), sem("ld_rt")
        k_zero, k_mask, k_spread, k_const = sem("k_zero"), sem("k_mask"), sem("k_spread"), sem("k_const")
        w_ps, w_sb, qs_sb, b3_sb, c_ps, c_sb, fk_ps, fk_sb, kv_ps, kv_sb = map(
            sem, ["w_ps", "w_sb", "qs_sb", "b3_sb", "c_ps", "c_sb", "fk_ps", "fk_sb", "kv_ps", "kv_sb"])
        x0t_ps, x0t_sb, qkv_ps, qkv_sb, pq_sb = map(
            sem, ["x0t_ps", "x0t_sb", "qkv_ps", "qkv_sb", "pq_sb"])
        score_sb, smax_sb, ssub_sb, exp_sb, ssum_sb, srec_sb, prob_sb, pv_sb = map(
            sem, ["score_sb", "smax_sb", "ssub_sb", "exp_sb", "ssum_sb", "srec_sb", "prob_sb", "pv_sb"])
        att_ps, att_t_sb, ao_ps = map(sem, ["att_ps", "att_t_sb", "ao_ps"])
        pq3_sb = sem("pq3_sb")
        st1_sb, mv1_sb, ve1_sb, rs1_sb, x1_sb = map(
            sem, ["st1_sb", "mv1_sb", "ve1_sb", "rs1_sb", "x1_sb"])
        x1t_ps, x1t_sb, fq_ps, fq_sb, xo_ps, den_sb, rden_sb = map(
            sem, ["x1t_ps", "x1t_sb", "fq_ps", "fq_sb", "xo_ps", "den_sb", "rden_sb"])
        r2_sb, st2_sb, mv2_sb, ve2_sb, rs2_sb, x2_sb, x2t_ps, x2t_sb = map(
            sem, ["r2_sb", "st2_sb", "mv2_sb", "ve2_sb", "rs2_sb", "x2_sb", "x2t_ps", "x2t_sb"])
        lg_ps, ltop_sb, leq_sb, lcand_sb, lfirst_sb, hot_sb, cum_sb, tsc_sb, sc_sb, rank_ps, rk_sb, rkh_sb, pos_sb = map(
            sem, ["lg_ps", "ltop_sb", "leq_sb", "lcand_sb", "lfirst_sb", "hot_sb", "cum_sb", "tsc_sb", "sc_sb",
                  "rank_ps", "rk_sb", "rkh_sb", "pos_sb"])
        scat, fill = sem("scat"), sem("fill")
        g_ps, sg_sb, gated_sb, hid_sb, sy_ps, rowb_sb = map(
            sem, ["g_ps", "sg_sb", "gated_sb", "hid_sb", "sy_ps", "rowb_sb"])
        cnt_ps, tab = sem("cnt_ps"), sem("tab")
        ld_slot = [sem(f"ld_slot{q}") for q in range(RING)]
        xst_ps, xst_sb, gu_ps, si_sb, ac_sb, act_ps, act_sb, y_ps = map(
            sem, ["xst_ps", "xst_sb", "gu_ps", "si_sb", "ac_sb", "act_ps", "act_sb", "y_ps"])
        r3_sb, st3_sb, mv3_sb, ve3_sb, rs3_sb, fin_sb = map(
            sem, ["r3_sb", "st3_sb", "mv3_sb", "ve3_sb", "rs3_sb", "fin_sb"])
        out_dma = [sem(f"out_dma{q}") for q in range(RING)]

        TAB_TAILS, TAB = 2, 13

        def tile_of(buf, c, s, w=D, row=None):
            row = w if row is None else row
            return buf[:, ds((c * S + s) * row, w)]

        def chunk_of(buf, c, w):
            return buf[:, ds(c * w, w)]

        def rows_part(c, at, w):
            return rows[:, c * S * RW:(c + 1) * S * RW].rearrange("p (s w) -> p s w", s=S)[:, :, at:at + w]

        def qkv_part(c, s, part, n=1):
            v = qkv[:, ds((c * S + s) * 3 * D, n * 3 * D)].rearrange("p (j w) -> p j w", w=3 * D)
            return v[:, :, part * D:(part + 1) * D]

        def shared_banks(c, h):
            return (0, 3) if c and h else (1, 2)

        SHARED_OUT = [0, 4, 5, 4]

        def pair_products(engine, c, i):
            return engine.tensor_tensor(pq[:, PB[i] * D:(PB[i] + i + 1) * D].rearrange("p (j d) -> p j d", d=D),
                                        qkv_part(c, 0, 1, i + 1), qkv_part(c, i, 0).to_broadcast([P, i + 1, D]), ALU.mult)

        block = ctx.enter_context(nc.Block())

        @block.sync
        def _(sp):
            sp.dma_start(x0[:, 0:CW].rearrange("p (s d) -> p s d", s=S), x_in[0]).then_inc(ld_x[0], 16)
            for n, w in ((2, "Wv"), (3, "Wo")):
                sp.dma_start(w_nat[:, n * P:(n + 1) * P], t[f"L0_attn_{w}"]).then_inc(ld_w, 16)
            for n, w in ((0, "bq"), (1, "bk")):
                sp.dma_start(bias[:, n * D:(n + 1) * D], t[f"L0_attn_{w}"].unsqueeze(0).to_broadcast([P, D])).then_inc(ld_bias, 16)
            for c in range(1, NC):
                sp.dma_start(x0[:, c * CW:(c + 1) * CW].rearrange("p (s d) -> p s d", s=S), x_in[c]).then_inc(ld_x[c], 16)
            sp.dma_start(gate[:], t["L0_ffn_gate_w"]).then_inc(ld_gate, 16)
            sp.dma_start(sh_gu[:, 0:I], t["L0_ffn_sh_gate"]).then_inc(ld_sh, 16)
            sp.dma_start(sh_gu[:, I:2 * I], t["L0_ffn_sh_up"]).then_inc(ld_sh, 16)
            sp.dma_start(sh_dn[:].rearrange("p (h d) -> p h d", h=HALVES),
                         t["L0_ffn_sh_down"].rearrange("(h p) d -> p h d", p=P)).then_inc(ld_sh, 16)
            gu = rt_gu[:].rearrange("p (e i) -> p e i", e=E)
            sp.dma_start(gu[:, :, 0:I], t["L0_ffn_rt_gate"].rearrange("e h i -> h e i")).then_inc(ld_rt, 16)
            sp.dma_start(gu[:, :, I:2 * I], t["L0_ffn_rt_up"].rearrange("e h i -> h e i")).then_inc(ld_rt, 16)
            sp.dma_start(rt_dn[:].rearrange("p (e h d) -> p e h d", e=E, h=HALVES),
                         t["L0_ffn_rt_down"].rearrange("e (h p) d -> p e h d", p=P)).then_inc(ld_rt, 16)
            sp.wait_ge(k_const, 1)
            sp.dma_start(table[FILLER:FILLER + P, :], filler[:]).then_inc(fill, 16)

            sp.wait_ge(tab, TAB_TAILS)
            tails = nc.values_load_multi_w_load_instructions(
                tail_row[0:1, :], engines=[mybir.EngineType.SP], min_val=0, max_val=FILLER - P,
                skip_runtime_bounds_check_because="rows worked out on the chip, inside the expert's region")[1]
            for row in tails:
                sp.dma_start(table[ds(row, P), :], filler[:]).then_inc(fill, 16)

            def round_of(b):
                return nc.values_load_multi_w_load_instructions(
                    blk_row[0:1, ds(b, RING)], engines=[mybir.EngineType.SP], min_val=0, max_val=FILLER,
                    skip_runtime_bounds_check_because="rows worked out on the chip, at most FILLER")[1]

            def load(row, q, used=None):
                if used is not None:
                    sp.wait_ge(r3_sb, used)
                sp.dma_start(slots[:, q * RW:(q + 1) * RW], table[ds(row, P), :]).then_inc(ld_slot[q], 16)

            sp.wait_ge(tab, TAB)
            first = round_of(0)
            sp.wait_ge(scat, 16 * NC * S)
            sp.wait_ge(fill, 16 * (E + 1))
            for q in range(RING):
                load(first[q], q)
            with sp.Fori(0, NBP // RING - 1) as k:
                after = round_of(RING * k + RING)
                for q in range(RING):
                    load(after[q], q, RING * k + q + 1)
            for q in range(RING):
                sp.wait_ge(ld_slot[q], 16 * (NBP // RING))
                sp.wait_ge(out_dma[q], 16 * ((NB - 1 - q) // RING + 1))

        @block.gpsimd
        def _(g):
            g.memset(ident[:], 0.0).then_inc(k_zero, 1)
            g.memset(ones16[:], 1.0).then_inc(k_zero, 1)
            g.wait_ge(k_zero, 2)
            g.affine_select(out=ident[:], in_=ident[:], compare_op=ALU.not_equal, fill=1.0, base=0,
                            pattern=[[-1, P]], channel_multiplier=1).then_inc(k_mask, 1)
            g.affine_select(out=before[:], in_=ones16[:], compare_op=ALU.is_gt, fill=0.0, base=0,
                            pattern=[[1, P]], channel_multiplier=-1).then_inc(k_mask, 1)
            g.memset(ctx1[:].rearrange("p (s w) -> p s w", s=S)[:, :, D:D + 1], 1.0)
            g.memset(score[:], -1e30)
            g.memset(upto[:], 1.0)
            g.memset(filler[:, 0:AT_TOKEN], 0.0)
            g.memset(filler[:, AT_TOKEN:RW].bitcast(I32), NOTOK)
            g.memset(mhalf[:], -0.5)
            g.memset(cum[:, 0:E], 0.0)
            for c in range(NC):
                col = rows_part(c, AT_TOKEN, 1)
                g.iota(col.bitcast(I32), pattern=[[BATCH, S], [1, 1]], base=c * P, channel_multiplier=1)
            g.iota(rev[:], pattern=[[-1, E]], base=E, channel_multiplier=0, allow_small_or_imprecise_dtypes=True)
            g.iota(region[:], pattern=[[ROWS, E]], base=0, channel_multiplier=0, allow_small_or_imprecise_dtypes=True)
            g.iota(kcol[:], pattern=[[P, KB]], base=0, channel_multiplier=0, allow_small_or_imprecise_dtypes=True)
            g.iota(bcol[:], pattern=[[1, NBP]], base=0, channel_multiplier=0, allow_small_or_imprecise_dtypes=True
                   ).then_inc(k_const, 1)
            g.wait_ge(k_const, 1)
            g.affine_select(out=upto[:], in_=upto[:], compare_op=ALU.is_ge, fill=0.0, base=0,
                            pattern=[[1, E], [-1, E]], channel_multiplier=0).then_inc(k_const, 1)

            def products(c):
                if c:
                    g.wait_ge(score_sb, 3 * c)
                for i in range(1, S - 1):
                    g.wait_ge(qkv_sb, S * c + i + 1)
                    pair_products(g, c, i).then_inc(pq_sb, 1)

            def rstd(n, c, mv_ready, ve_done, rs_done):
                g.wait_ge(mv_ready, S * c + S)
                at = (c * 2 + n) * S
                var = mv[:, at * 2:(at + S) * 2].rearrange("p (s w) -> p s w", w=2)[:, :, 1:2]
                g.tensor_scalar(ve[:, at:at + S], var, EPS_LN, None, ALU.add).then_inc(ve_done, 1)
                g.wait_ge(ve_done, c + 1)
                g.tensor_tensor(rs[:, at:at + S], ve[:, at:at + S], mhalf[:], ALU.pow).then_inc(rs_done, 1)

            def count(c):
                g.wait_ge(hot_sb, c + 1)
                for s in range(S):
                    at = c * S + s
                    if at:
                        g.wait_ge(cum_sb, at)
                    g.tensor_tensor(cum[:, (at + 1) * E:(at + 2) * E], cum[:, at * E:(at + 1) * E],
                                    hot[:, at * E:(at + 1) * E], ALU.add).then_inc(cum_sb, 1)

            def score_of(c):
                g.wait_ge(tsc_sb, c + 1)
                g.tensor_scalar(rows_part(c, AT_SCORE, 1), chunk_of(tsc, c, S).unsqueeze(2), 0.5, 0.5, ALU.mult, ALU.add).then_inc(sc_sb, 1)

            def scatter(c):
                g.wait_ge(pos_sb, c + 1)
                g.wait_ge(sc_sb, c + 1)
                for s in range(S):
                    if s % 2 == 0:
                        g.wait_ge(rowb_sb, 2 * c + s // 2 + 1)
                    g.indirect_dma_start(
                        out=table[:, :],
                        out_offset=bass.IndirectOffsetOnAxis(ap=pos[:, c * S + s:c * S + s + 1], axis=0),
                        in_=tile_of(rows, c, s, RW), in_offset=None).then_inc(scat, 16)

            for tick in range(NC + 2):
                c_a, c_b, c_c = tick, tick - 1, tick - 2
                if c_a < NC:
                    products(c_a)
                if c_c >= 0:
                    rstd(1, c_c, mv2_sb, ve2_sb, rs2_sb)
                if 0 <= c_b < NC:
                    rstd(0, c_b, mv1_sb, ve1_sb, rs1_sb)
                if tick == NC + 1:
                    scatter(1)
                if c_c >= 0:
                    count(c_c)
                    score_of(c_c)
                if tick == NC:
                    scatter(0)
            for c in range(2, NC):
                scatter(c)

            def rstd3(b, r):
                g.wait_ge(ve3_sb, b + 1)
                g.tensor_tensor(rs3[:, r:r + 1], ve3[:, r:r + 1], mhalf[:, 0:1], ALU.pow).then_inc(rs3_sb, 1)

            last_token = g.to_reg(TOK - 1)

            def send(r):
                g.indirect_dma_start(
                    out=out_rows, out_offset=bass.IndirectOffsetOnAxis(ap=token[:, r:r + 1], axis=0),
                    in_=fin[:, r * D:(r + 1) * D], in_offset=None,
                    bounds_check=last_token, oob_is_err=False).then_inc(out_dma[r], 16)

            rstd3(0, 0)
            with g.Fori(0, (NB - 5) // RING) as k:
                for r in range(RING):
                    rstd3(RING * k + r + 1, (r + 1) % RING)
                    send(r)
            for b in range(NB - 5, NB):
                if b + 1 < NB:
                    rstd3(b + 1, (b + 1) % RING)
                g.wait_ge(fin_sb, b + 1)
                send(b % RING)

        @block.scalar
        def _(a):
            a.dma_start(beta[:], t["L0_attn_beta"].unsqueeze(0).to_broadcast([P, HEADS])).then_inc(ld_beta, 16)
            for n, w in ((0, "Wq"), (1, "Wk")):
                a.dma_start(w_nat[:, n * P:(n + 1) * P], t[f"L0_attn_{w}"]).then_inc(ld_w, 16)
            for n, w in ((2, "bv"), (3, "bo")):
                a.dma_start(bias[:, n * D:(n + 1) * D], t[f"L0_attn_{w}"].unsqueeze(0).to_broadcast([P, D])).then_inc(ld_bias, 16)
            a.wait_ge(ld_beta, 16)
            a.activation(qscale[:], beta[:], ACT.Exp, scale=-1.0).then_inc(qs_sb, 1)
            a.dma_start(ctx1[:].rearrange("p (s w) -> p s w", s=S)[:, :, 0:D],
                        t["ctx_1024"].rearrange("s l d -> l s d")).then_inc(ld_ctx, 16)
            a.dma_start(proj[:], t["L0_xattn_projection"]).then_inc(ld_proj, 16)
            a.wait_ge(w_ps, 1)
            a.copy(w_t[:, D:4 * D], bank[3][:, D:4 * D]).then_inc(w_sb, 1)

            def copy_x0t(c):
                a.wait_ge(x0t_ps, c + 1)
                a.copy(chunk_of(x0_t, c, CW), bank[0][:]).then_inc(x0t_sb, 1)

            def copy_qkv(c, s):
                a.wait_ge(qkv_ps, S * c + s + 1)
                a.copy(qkv[:, (c * S + s) * 3 * D:(c * S + s + 1) * 3 * D], bank[1 + s % 2][:, 0:3 * D]).then_inc(qkv_sb, 1)

            def exps(c):
                a.wait_ge(ssub_sb, c + 1)
                a.activation(chunk_of(prob, c, SW), chunk_of(ssub, c, SW), ACT.Exp).then_inc(exp_sb, 1)

            def copy_att(c):
                a.wait_ge(att_ps, c + 1)
                if c:
                    a.wait_ge(ao_ps, c)
                a.copy(att_t[:], bank[0][:]).then_inc(att_t_sb, 1)

            def copy_x1t(c):
                a.wait_ge(x1t_ps, c + 1)
                a.copy(x1_t[:], bank[4][:]).then_inc(x1t_sb, 1)

            def features_q(c):
                a.wait_ge(fq_ps, c + 1)
                if c:
                    a.wait_ge(xo_ps, c)
                a.activation(rf_q[:], bank[4][0:M, :], ACT.Exp, scale=INV_SQRT_D).then_inc(fq_sb, 1)

            def copy_x2t(c):
                a.wait_ge(x2t_ps, c + 1)
                a.copy(chunk_of(x2_t, c, CW), bank[7][:]).then_inc(x2t_sb, 1)

            def score_tanh(c):
                a.wait_ge(ltop_sb, c + 1)
                a.activation(chunk_of(tsc, c, S), chunk_of(ltop, c, S), ACT.Tanh, scale=0.5).then_inc(tsc_sb, 1)

            def shared_tanh(c, h):
                a.wait_ge(g_ps, 2 * c + h + 1)
                a.activation(sg[:, h * CW:(h + 1) * CW], bank[shared_banks(c, h)[0]][:], ACT.Tanh, scale=0.5
                             ).then_inc(sg_sb, 1)

            copy_x0t(0)
            for s in range(S):
                copy_qkv(0, s)
            for tick in range(NC + 2):
                c_a, c_b, c_c = tick, tick - 1, tick - 2
                if tick == 0:
                    a.wait_ge(fk_ps, 1)
                    a.activation(rf_k[:], bank[6][0:CTX, 0:S * M], ACT.Exp, scale=INV_SQRT_D).then_inc(fk_sb, 1)
                if 0 <= c_b < NC:
                    copy_att(c_b)
                if c_a + 1 < NC:
                    copy_x0t(c_a + 1)
                if c_a < 2:
                    exps(c_a)
                if c_a + 1 < NC:
                    for s in range(3):
                        copy_qkv(c_a + 1, s)
                        if c_a == 2 and s == 0:
                            exps(c_a)
                if c_a == NC - 1:
                    exps(c_a)
                if tick == NC - 1 or tick == NC:
                    shared_tanh(tick - (NC - 1), 0)
                if tick == NC + 1:
                    shared_tanh(2, 0)
                    shared_tanh(2, 1)
                if c_c >= 0:
                    copy_x2t(c_c)
                if c_a + 1 < NC:
                    copy_qkv(c_a + 1, 3)
                if 0 <= c_b < NC:
                    copy_x1t(c_b)
                    features_q(c_b)
                if c_c >= 0:
                    score_tanh(c_c)
                if tick == NC - 1 or tick == NC:
                    shared_tanh(tick - (NC - 1), 1)
            for h in range(HALVES):
                shared_tanh(3, h)

            a.activation(silu_warm[:], qscale[0:1, 0:1], ACT.Silu)

            def copy_xst(b, q):
                a.wait_ge(xst_ps, b + 1)
                a.copy(xs_t[:, q * D:(q + 1) * D], bank[q][:, 0:D]).then_inc(xst_sb, 1)

            def silu(b, q, r):
                a.wait_ge(gu_ps, b + 1)
                a.activation(si[:, q * I:(q + 1) * I], bank[2 + q][:, 0:I], ACT.Silu,
                             scale=slots[:, r * RW + AT_SCORE:r * RW + AT_SCORE + 1]).then_inc(si_sb, 1)

            def copy_act(b, q):
                a.wait_ge(act_ps, b + 1)
                a.copy(ac_t[:, q * I:(q + 1) * I], bank[4 + q][:, 0:I]).then_inc(act_sb, 1)

            def step(b, r, more=2):
                if more > 1:
                    copy_xst(b + 2, r % 2)
                if more > 0:
                    silu(b + 1, (r + 1) % 2, (r + 1) % RING)
                copy_act(b, r % 2)

            copy_xst(0, 0)
            copy_xst(1, 1)
            silu(0, 0, 0)
            with a.Fori(0, (NB - 5) // RING) as k:
                for r in range(RING):
                    step(RING * k + r, r)
            for b in range(NB - 5, NB):
                step(b, b % RING, NB - 1 - b)

        @block.vector
        def _(v):
            v.wait_ge(k_const, 1)
            v.memset(spread[:], 0.0).then_inc(k_spread, 1)
            v.wait_ge(k_spread, 1)
            for part in range(3):
                v.memset(spread[32 * part:32 * part + 1, :], 1.0).then_inc(k_spread, 1)
            scale_b = qscale[:].unsqueeze(2).to_broadcast([P, HEADS, DH])
            heads = lambda ap: ap.rearrange("p (h d) -> p h d", h=HEADS)
            v.wait_ge(ld_bias, 64)
            v.wait_ge(qs_sb, 1)
            v.scalar_tensor_tensor(heads(bias[:, 0:D]), heads(bias[:, 0:D]), INV_SQRT_DH, scale_b,
                                   ALU.mult, ALU.mult).then_inc(b3_sb, 1)
            v.wait_ge(w_ps, 1)
            v.scalar_tensor_tensor(heads(w_t[:, 0:D]), heads(bank[0][:, 0:D]), INV_SQRT_DH, scale_b,
                                   ALU.mult, ALU.mult).then_inc(w_sb, 1)
            with nc.allow_low_precision(reason="the three parts add up to the float32 bias"):
                v.wait_ge(b3_sb, 1)
                v.tensor_copy(bias3[:], bias[0:65, :]).then_inc(b3_sb, 1)
                v.wait_ge(b3_sb, 2)
                v.tensor_tensor(brest[:], bias[0:65, :], bias3[:], ALU.subtract).then_inc(b3_sb, 1)
                v.wait_ge(b3_sb, 3)
                v.tensor_copy(bias3[32:33, :], brest[32:33, :]).then_inc(b3_sb, 1)
                v.tensor_copy(bias3[64:65, :], brest[64:65, :]).then_inc(b3_sb, 1)
                v.wait_ge(b3_sb, 5)
                v.tensor_tensor(bias3[64:65, :], brest[64:65, :], bias3[64:65, :], ALU.subtract).then_inc(b3_sb, 1)

            def products3(c):
                v.wait_ge(qkv_sb, S * c + S)
                if c:
                    v.wait_ge(score_sb, 3 * c)
                pair_products(v, c, S - 1).then_inc(pq3_sb, 1)

            def scores(c):
                for i in range(1, S):
                    if i < S - 1:
                        v.wait_ge(pq_sb, 2 * c + i)
                    else:
                        v.wait_ge(pq3_sb, c + 1)
                    at = c * SW + (i - 1) * S * HEADS
                    v.tensor_reduce(score[:, at:at + (i + 1) * HEADS],
                                    pq[:, PB[i] * D:(PB[i] + i + 1) * D].rearrange("p (g d) -> p g d", d=DH),
                                    X, ALU.add).then_inc(score_sb, 1)

            def by_query(ap):
                return ap.rearrange("p (i j h) -> p i h j", i=S - 1, j=S)

            SQ = (S - 1) * HEADS

            def over_keys(ap):
                return ap.rearrange("p (i h) -> p i h", i=S - 1).unsqueeze(3).to_broadcast([P, S - 1, HEADS, S])

            def softmax_max(c):
                v.wait_ge(score_sb, 3 * c + 3)
                v.tensor_reduce(chunk_of(smax, c, SQ), by_query(chunk_of(score, c, SW)), X, ALU.max).then_inc(smax_sb, 1)

            def softmax_sub(c):
                v.wait_ge(smax_sb, c + 1)
                v.tensor_tensor(by_query(chunk_of(ssub, c, SW)), by_query(chunk_of(score, c, SW)),
                                over_keys(chunk_of(smax, c, SQ)), ALU.subtract).then_inc(ssub_sb, 1)

            def softmax_sum(c):
                v.wait_ge(exp_sb, c + 1)
                v.tensor_reduce(chunk_of(ssum, c, SQ), by_query(chunk_of(prob, c, SW)), X, ALU.add).then_inc(ssum_sb, 1)
                v.wait_ge(ssum_sb, c + 1)
                v.reciprocal(chunk_of(srec, c, SQ), chunk_of(ssum, c, SQ)).then_inc(srec_sb, 1)
                v.wait_ge(srec_sb, c + 1)
                v.tensor_tensor(by_query(chunk_of(prob, c, SW)), by_query(chunk_of(prob, c, SW)),
                                over_keys(chunk_of(srec, c, SQ)), ALU.mult).then_inc(prob_sb, 1)

            def attend(c):
                v.wait_ge(prob_sb, c + 1)
                if c:
                    v.wait_ge(att_ps, c)
                for i in range(1, S):
                    n = (i + 1) * HEADS
                    at = c * SW + (i - 1) * S * HEADS
                    p = prob[:, at:at + n].rearrange("p (j h) -> p j h", h=HEADS)
                    v.tensor_tensor(
                        pv[:, PB[i] * D:(PB[i] + i + 1) * D].rearrange("p (j h d) -> p j h d", h=HEADS, d=DH),
                        qkv_part(c, 0, 2, i + 1).rearrange("p j (h d) -> p j h d", d=DH),
                        p.unsqueeze(3).to_broadcast([P, i + 1, HEADS, DH]), ALU.mult).then_inc(pv_sb, 1)

            def stats(n, c, src, st_done, mv_done):
                for s in range(S):
                    at = (c * 2 + n) * S + s
                    v.bn_stats(st[:, at * 6:(at + 1) * 6], src[:, s * D:(s + 1) * D]).then_inc(st_done, 1)
                for s in range(S):
                    at = (c * 2 + n) * S + s
                    v.wait_ge(st_done, S * c + s + 1)
                    v.bn_aggr(mv[:, at * 2:(at + 1) * 2], st[:, at * 6:(at + 1) * 6]).then_inc(mv_done, 1)

            def stats1(c):
                v.wait_ge(ao_ps, c + 1)
                stats(0, c, bank[3], st1_sb, mv1_sb)

            def stats2(c):
                v.wait_ge(r2_sb, 2 * c + 2)
                stats(1, c, r2, st2_sb, mv2_sb)

            def normed(n, c, src, dst, row, rs_ready, done):
                v.wait_ge(rs_ready, c + 1)
                for s in range(S):
                    at = (c * 2 + n) * S + s
                    v.tensor_scalar(dst[:, (c * S + s) * row:(c * S + s) * row + D], src[:, s * D:(s + 1) * D],
                                    mv[:, at * 2:at * 2 + 1], rs[:, at:at + 1], ALU.subtract, ALU.mult).then_inc(done, 1)

            def residual2(c):
                at = c * S
                v.wait_ge(xo_ps, c + 1)
                for h in range(2):
                    z = bank[5 + h][:].rearrange("p (s w) -> p s w", s=2)[:, :, D:D + 1]
                    v.tensor_scalar(den[:, at + 2 * h:at + 2 * h + 2].unsqueeze(2), z, EPS_X, None, ALU.add).then_inc(den_sb, 1)
                v.wait_ge(den_sb, 2 * c + 2)
                v.reciprocal(rden[:, at:at + S], den[:, at:at + S]).then_inc(rden_sb, 1)
                if c:
                    v.wait_ge(x2_sb, S * c)
                v.wait_ge(rden_sb, c + 1)
                for h in range(2):
                    for n in range(2):
                        s = 2 * h + n
                        last = v.scalar_tensor_tensor(
                            r2[:, s * D:(s + 1) * D], bank[5 + h][:, n * 256:n * 256 + D],
                            rden[:, at + s:at + s + 1], tile_of(x1, c, s), ALU.mult, ALU.add)
                    last.then_inc(r2_sb, 1)

            def route(c):
                by_tile = lambda ap: ap.rearrange("p (s e) -> p s e", s=S)
                over_e = lambda ap: ap.unsqueeze(2).to_broadcast([P, S, E])
                lg = by_tile(bank[7][:, 0:S * E])
                W = S * E
                v.wait_ge(lg_ps, c + 1)
                v.tensor_reduce(chunk_of(ltop, c, S), lg, X, ALU.max).then_inc(ltop_sb, 1)
                v.wait_ge(ltop_sb, c + 1)
                v.tensor_tensor(by_tile(chunk_of(leq, c, W)), lg, over_e(chunk_of(ltop, c, S)), ALU.is_equal).then_inc(leq_sb, 1)
                v.wait_ge(leq_sb, c + 1)
                v.tensor_tensor(by_tile(chunk_of(lcand, c, W)), by_tile(chunk_of(leq, c, W)),
                                rev[:].unsqueeze(1).to_broadcast([P, S, E]), ALU.mult).then_inc(lcand_sb, 1)
                v.wait_ge(lcand_sb, c + 1)
                v.tensor_reduce(chunk_of(lfirst, c, S), by_tile(chunk_of(lcand, c, W)), X, ALU.max).then_inc(lfirst_sb, 1)
                v.wait_ge(lfirst_sb, c + 1)
                v.tensor_tensor(by_tile(chunk_of(hot, c, W)), by_tile(chunk_of(lcand, c, W)),
                                over_e(chunk_of(lfirst, c, S)), ALU.is_equal).then_inc(hot_sb, 1)

            def place(c):
                by_tile = lambda ap: ap.rearrange("p (s e) -> p s e", s=S)
                W = S * E
                v.wait_ge(rank_ps, c + 1)
                v.tensor_tensor(by_tile(chunk_of(rk, c, W)), by_tile(bank[7][:, 0:W]),
                                region[:].unsqueeze(1).to_broadcast([P, S, E]), ALU.add).then_inc(rk_sb, 1)
                v.wait_ge(rk_sb, c + 1)
                v.tensor_tensor(chunk_of(rkh, c, W), chunk_of(rk, c, W), chunk_of(hot, c, W), ALU.mult).then_inc(rkh_sb, 1)
                v.wait_ge(rkh_sb, c + 1)
                with nc.allow_low_precision(reason="row numbers are whole and under 2**24: exact in float32"):
                    v.tensor_reduce(chunk_of(pos, c, S), by_tile(chunk_of(rkh, c, W)), X, ALU.add).then_inc(pos_sb, 1)

            def shared_hidden(c, h):
                g_bank, u_bank = shared_banks(c, h)
                v.wait_ge(sg_sb, 2 * c + h + 1)
                v.scalar_tensor_tensor(sg[:, h * CW:(h + 1) * CW], sg[:, h * CW:(h + 1) * CW], 1.0, bank[g_bank][:],
                                       ALU.add, ALU.mult).then_inc(gated_sb, 1)
                if c >= 2:
                    v.wait_ge(sy_ps, c - 1)
                at = ((c % 2) * HALVES + h) * CW
                v.wait_ge(gated_sb, 2 * c + h + 1)
                v.tensor_tensor(hid[:, at:at + CW], sg[:, h * CW:(h + 1) * CW], bank[u_bank][:], ALU.mult
                                ).then_inc(hid_sb, 1)

            def shared_out(c):
                v.wait_ge(sy_ps, c + 1)
                for h in range(2):
                    v.scalar_tensor_tensor(
                        rows_part(c, AT_BASE, D)[:, 2 * h:2 * h + 2, :],
                        bank[SHARED_OUT[c]][:, h * 2 * D:(h + 1) * 2 * D].rearrange("p (s d) -> p s d", s=2), 0.5,
                        rows_part(c, 0, D)[:, 2 * h:2 * h + 2, :], ALU.mult, ALU.add).then_inc(rowb_sb, 1)

            for tick in range(NC + 2):
                c_a, c_b, c_c = tick, tick - 1, tick - 2
                if tick == 0:
                    v.wait_ge(c_ps, 1)
                    v.tensor_copy(proj_t[:], bank[5][:, 0:M]).then_inc(c_sb, 1)
                    v.tensor_copy(ctx_t[:], bank[5][:, M:M + S * CTX]).then_inc(c_sb, 1)
                if c_c >= 0:
                    residual2(c_c)
                    stats2(c_c)
                if c_c >= 1:
                    place(c_c - 1)
                if c_a < NC:
                    products3(c_a)
                    scores(c_a)
                if tick == NC:
                    stats1(c_b)
                if tick == NC + 1:
                    shared_hidden(2, 0)
                if c_c >= 0:
                    normed(1, c_c, r2, rows, RW, rs2_sb, x2_sb)
                if c_a < NC:
                    softmax_max(c_a)
                    softmax_sub(c_a)
                if 0 <= c_b < NC and tick < NC:
                    stats1(c_b)
                if tick == NC - 1:
                    shared_hidden(0, 0)
                if tick == NC:
                    shared_out(0)
                if tick == NC + 1:
                    shared_out(1)
                    shared_hidden(2, 1)
                if tick == 0:
                    v.wait_ge(kv_ps, 1)
                    for n in range(2):
                        v.tensor_scalar(kvz[:, 2 * n * (D + 1):2 * (n + 1) * (D + 1)].rearrange("p (s w) -> p s w", s=2),
                                        bank[6 + n][0:M, :].rearrange("p (s w) -> p s w", s=2)[:, :, 0:D + 1],
                                        1.0 / math.sqrt(M), None, ALU.mult).then_inc(kv_sb, 1)
                if c_a < NC:
                    softmax_sum(c_a)
                if 0 <= c_b < NC:
                    normed(0, c_b, bank[3], x1, D, rs1_sb, x1_sb)
                if c_a < NC:
                    attend(c_a)
                if tick == NC:
                    shared_hidden(1, 0)
                if c_c >= 0:
                    route(c_c)
                if tick == NC - 1 or tick == NC:
                    shared_hidden(tick - (NC - 1), 1)
            shared_hidden(3, 0)
            shared_out(2)
            place(NC - 1)

            step = [0]

            def tabled(ins):
                step[0] += 1
                ins.then_inc(tab, 1)
                v.wait_ge(tab, step[0])

            shared_hidden(3, 1)
            v.wait_ge(cnt_ps, 1)
            v.wait_ge(k_const, 2)
            tabled(v.tensor_copy(cnt[:], bank[7][0:1, 0:E]))
            tabled(v.tensor_tensor(tail_row[:], cnt[:], region[0:1, :], ALU.add))
            g3 = gtk[:].rearrange("p (e k) -> p e k", e=E)
            tabled(v.tensor_tensor(g3, cnt[:].unsqueeze(2).to_broadcast([1, E, KB]),
                                   kcol[:].unsqueeze(1).to_broadcast([1, E, KB]), ALU.is_gt))
            tabled(v.tensor_reduce(nblk[:], g3, X, ALU.add))
            m3 = nmask[:].rearrange("p (e f) -> p e f", e=E)
            tabled(v.tensor_tensor(m3, upto[:].rearrange("p (e f) -> p e f", e=E),
                                   nblk[:].unsqueeze(1).to_broadcast([1, E, E]), ALU.mult))
            tabled(v.tensor_reduce(cblk[:], m3, X, ALU.add))
            shared_out(3)
            tabled(v.tensor_scalar(dstep[:], nblk[:], -float(P), float(ROWS), ALU.mult, ALU.add))
            ge3 = ge[:].rearrange("p (b e) -> p b e", e=E)
            ged3 = ged[:].rearrange("p (b e) -> p b e", e=E)
            tabled(v.tensor_tensor(ge3, bcol[:].unsqueeze(2).to_broadcast([1, NBP, E]),
                                   cblk[:].unsqueeze(1).to_broadcast([1, NBP, E]), ALU.is_ge))
            tabled(v.tensor_tensor(ged3, ge3, dstep[:].unsqueeze(1).to_broadcast([1, NBP, E]), ALU.mult))
            tabled(v.tensor_reduce(rsum[:], ged3, X, ALU.add))
            tabled(v.scalar_tensor_tensor(radd[:], bcol[:], float(P), rsum[:], ALU.mult, ALU.add))
            tabled(v.tensor_scalar(blk_row[:], radd[:], float(FILLER), None, ALU.min))
            v.tensor_reduce(esum[:], ge3, X, ALU.add).then_inc(tab, 1)
            v.wait_ge(tab, TAB)
            v.tensor_scalar(blk_e[:], esum[:], float(E - 1), None, ALU.min).then_inc(tab, 1)
            def gated(b, q, r):
                v.wait_ge(si_sb, b + 1)
                v.scalar_tensor_tensor(ac[:, q * I:(q + 1) * I], bank[2 + q][:, I:2 * I],
                                       slots[:, r * RW + AT_SCORE:r * RW + AT_SCORE + 1], si[:, q * I:(q + 1) * I],
                                       ALU.mult, ALU.mult).then_inc(ac_sb, 1)

            def residual3(b, q, r, nth):
                v.wait_ge(y_ps, b + 1)
                if nth is not None:
                    v.wait_ge(out_dma[r], 16 * nth)
                v.tensor_copy(token[:, r:r + 1], slots[:, r * RW + AT_TOKEN:(r + 1) * RW].bitcast(I32))
                v.tensor_tensor(r3[:, r * D:(r + 1) * D], bank[6 + q][:, 0:D],
                                slots[:, r * RW + AT_BASE:r * RW + AT_BASE + D], ALU.add).then_inc(r3_sb, 1)

            def stats3(b, r):
                v.wait_ge(r3_sb, b + 1)
                v.bn_stats(st3[:, r * 6:(r + 1) * 6], r3[:, r * D:(r + 1) * D]).then_inc(st3_sb, 1)

            def aggr3(b, r):
                v.bn_aggr(mv3[:, 2 * r:2 * r + 2], st3[:, r * 6:(r + 1) * 6]).then_inc(mv3_sb, 1)

            def var3(b, r):
                v.wait_ge(mv3_sb, b + 1)
                v.tensor_scalar(ve3[:, r:r + 1], mv3[:, 2 * r + 1:2 * r + 2], EPS_LN, None, ALU.add).then_inc(ve3_sb, 1)

            def normed3(b, r):
                v.wait_ge(rs3_sb, b + 1)
                v.tensor_scalar(fin[:, r * D:(r + 1) * D], r3[:, r * D:(r + 1) * D], mv3[:, 2 * r:2 * r + 1],
                                rs3[:, r:r + 1], ALU.subtract, ALU.mult).then_inc(fin_sb, 1)

            def step3(b, r, nth, gate_next=True, norm_last=True):
                if gate_next:
                    gated(b + 2, r % 2, (r + 2) % RING)
                residual3(b, r % 2, r, nth)
                stats3(b, r)
                v.wait_ge(st3_sb, b + 1)
                if norm_last:
                    normed3(b - 1, (r - 1) % RING)
                aggr3(b, r)
                var3(b, r)

            gated(0, 0, 0)
            gated(1, 1, 1)
            for b in range(RING):
                step3(b, b, None, norm_last=b > 0)
            LOOPS = (NB - 5) // RING
            with v.Fori(0, LOOPS - 1) as k:
                for r in range(RING):
                    step3(RING * k + RING + r, r, k + 1)
            for b in range(RING * LOOPS, NB):
                step3(b, b % RING, b // RING, gate_next=b + 2 < NB)
            normed3(NB - 1, (NB - 1) % RING)

        @block.tensor
        def _(pe):
            pe.wait_ge(k_mask, 2)
            pe.wait_ge(ld_w, 64)
            pe.transpose(bank[0][:, 0:P], w_nat[:, 0:P], ident[:])
            for n in range(1, 4):
                last = pe.transpose(bank[3][:, n * P:(n + 1) * P], w_nat[:, n * P:(n + 1) * P], ident[:])
            last.then_inc(w_ps, 1)

            def x0_transposes(c):
                pe.wait_ge(ld_x[c], 16)
                if c == 0:
                    pe.wait_ge(w_sb, 2)
                elif c == 1:
                    pe.wait_ge(x0t_sb, 1)
                else:
                    pe.wait_ge(att_t_sb, c - 1)
                for s in range(S):
                    last = pe.transpose(bank[0][:, s * D:(s + 1) * D], tile_of(x0, c, s), ident[:])
                last.then_inc(x0t_ps, 1)

            def project(c, s):
                pe.wait_ge(x0t_sb, c + 1)
                n = S * c + s
                if n >= 2:
                    pe.wait_ge(qkv_sb, n - 1)
                pe.matmul(bank[1 + s % 2][:, 0:3 * D], tile_of(x0_t, c, s), w_t[:, 0:3 * D], start=True, stop=False)
                if n == 0:
                    pe.wait_ge(b3_sb, 6)
                    pe.wait_ge(k_spread, 4)
                pe.matmul(bank[1 + s % 2][:, 0:3 * D], spread[:], bias3[:, 0:3 * D], start=False, stop=True
                          ).then_inc(qkv_ps, 1)

            def att_transposes(c, first, last_i):
                pe.wait_ge(x0t_sb, min(c + 2, NC))
                pe.wait_ge(qkv_sb, S * c + 1)
                if first == 0:
                    v0 = qkv[:, c * S * 3 * D + 2 * D:c * S * 3 * D + 3 * D]
                    pe.matmul(bank[0][:, 0:D], v0, ident[:], start=True, stop=True)
                for i in range(max(first, 1), last_i + 1):
                    pe.wait_ge(pv_sb, 3 * c + i)
                    for j in range(i + 1):
                        at = (PB[i] + j) * D
                        last = pe.matmul(bank[0][:, i * D:(i + 1) * D], pv[:, at:at + D], ident[:],
                                         start=j == 0, stop=j == i)
                if last_i == S - 1:
                    last.then_inc(att_ps, 1)

            def att_out(c):
                pe.wait_ge(att_t_sb, c + 1)
                if c:
                    pe.wait_ge(x1_sb, S * c)
                for s in range(S):
                    o = bank[3][:, s * D:(s + 1) * D]
                    pe.matmul(o, att_t[:, s * D:(s + 1) * D], w_t[:, 3 * D:4 * D], start=True, stop=False)
                    pe.matmul(o, tile_of(x0_t, c, s), ident[:], start=False, stop=False)
                    last = pe.matmul(o, spread[:], bias3[:, 3 * D:4 * D], start=False, stop=True)
                last.then_inc(ao_ps, 1)

            def x1_transposes(c):
                pe.wait_ge(x1_sb, S * c + S)
                if c:
                    pe.wait_ge(fq_sb, c)
                for s in range(S):
                    last = pe.transpose(bank[4][:, s * D:(s + 1) * D], tile_of(x1, c, s), ident[:])
                last.then_inc(x1t_ps, 1)

            def features(c):
                pe.wait_ge(x1t_sb, c + 1)
                pe.matmul(bank[4][0:M, :], proj_t[:], x1_t[:], start=True, stop=True).then_inc(fq_ps, 1)

            def cross_out(c):
                pe.wait_ge(fq_sb, c + 1)
                if c:
                    pe.wait_ge(r2_sb, 2 * c)
                else:
                    pe.wait_ge(kv_sb, 2)
                for s in range(S):
                    last = pe.matmul(bank[5 + s // 2][:, (s % 2) * 256:(s % 2) * 256 + D + 1], rf_q[:, s * D:(s + 1) * D],
                                     kvz[:, s * (D + 1):(s + 1) * (D + 1)], start=True, stop=True)
                last.then_inc(xo_ps, 1)

            def x2_transposes(c):
                pe.wait_ge(x2_sb, S * c + S)
                if c:
                    pe.wait_ge(pos_sb, c)
                for s in range(S):
                    last = pe.transpose(bank[7][:, s * D:(s + 1) * D], tile_of(rows, c, s, D, RW), ident[:])
                last.then_inc(x2t_ps, 1)

            def logits(c):
                pe.wait_ge(x2t_sb, c + 1)
                for s in range(S):
                    last = pe.matmul(bank[7][:, s * E:(s + 1) * E], tile_of(x2_t, c, s), gate[:], start=True, stop=True)
                last.then_inc(lg_ps, 1)

            def rank(c):
                pe.wait_ge(hot_sb, c + 1)
                pe.wait_ge(cum_sb, S * c + S)
                W = S * E
                pe.matmul(bank[7][:, 0:W], before[:], chunk_of(hot, c, W), start=True, stop=False)
                pe.matmul(bank[7][:, 0:W], ones16[:], chunk_of(cum, c, W), start=False, stop=True).then_inc(rank_ps, 1)

            def shared_up(c, h):
                g_bank, u_bank = shared_banks(c, h)
                pe.wait_ge(x2t_sb, c + 1)
                if (c, h) == (0, 0):
                    pe.wait_ge(ld_sh, 48)
                    pe.wait_ge(qkv_sb, NC * S)
                elif (c, h) == (1, 1):
                    pe.wait_ge(x1_sb, NC * S)
                    pe.wait_ge(rowb_sb, 2)
                elif c < 2:
                    pe.wait_ge(hid_sb, 2 * c + h)
                else:
                    pe.wait_ge(hid_sb, 2 * c + h - 1)
                pe.matmul(bank[u_bank][:], sh_gu[:, I + h * P:I + (h + 1) * P], chunk_of(x2_t, c, CW),
                          start=True, stop=True)
                pe.matmul(bank[g_bank][:], sh_gu[:, h * P:(h + 1) * P], chunk_of(x2_t, c, CW),
                          start=True, stop=True).then_inc(g_ps, 1)

            def shared_down(c):
                pe.wait_ge(hid_sb, 2 * c + 2)
                if c == 0:
                    pe.wait_ge(att_t_sb, NC)
                elif c == 1:
                    pe.wait_ge(fq_sb, NC)
                elif c == 2:
                    pe.wait_ge(r2_sb, 2 * NC)
                else:
                    pe.wait_ge(rowb_sb, 4)
                for s in range(S):
                    for h in range(HALVES):
                        at = ((c % 2) * HALVES + h) * CW + s * D
                        last = pe.matmul(bank[SHARED_OUT[c]][:, s * D:(s + 1) * D], hid[:, at:at + D],
                                         sh_dn[:, h * D:(h + 1) * D], start=h == 0, stop=h == HALVES - 1)
                last.then_inc(sy_ps, 1)

            x0_transposes(0)
            for s in range(S):
                project(0, s)
            for tick in range(NC + 2):
                c_a, c_b, c_c = tick, tick - 1, tick - 2
                if tick == 0:
                    pe.wait_ge(ld_ctx, 16)
                    pe.wait_ge(ld_proj, 16)
                    pe.wait_ge(k_const, 1)
                    pe.transpose(bank[5][:, 0:M], proj[:], ident[0:M, 0:M])
                    c3 = ctx1[:].rearrange("p (s w) -> p s w", s=S)
                    for s in range(S):
                        last = pe.transpose(bank[5][:, M + s * CTX:M + (s + 1) * CTX], c3[:, s, 0:D], ident[0:CTX, 0:CTX])
                    last.then_inc(c_ps, 1)
                    pe.wait_ge(c_sb, 2)
                    for s in range(S):
                        last = pe.matmul(bank[6][0:CTX, s * M:(s + 1) * M], ctx_t[:, s * CTX:(s + 1) * CTX], proj_t[:],
                                         start=True, stop=True)
                    last.then_inc(fk_ps, 1)
                    pe.wait_ge(fk_sb, 1)
                    for s in range(S):
                        last = pe.matmul(bank[6 + s // 2][0:M, (s % 2) * 256:(s % 2) * 256 + D + 1],
                                         rf_k[:, s * M:(s + 1) * M],
                                         ctx1[:, s * (D + 1):(s + 1) * (D + 1)], start=True, stop=True)
                    last.then_inc(kv_ps, 1)
                    pe.wait_ge(ld_gate, 16)
                if 0 <= c_b < NC:
                    att_transposes(c_b, 0, 1)
                if c_c >= 0:
                    cross_out(c_c)
                if 0 <= c_b < NC:
                    att_transposes(c_b, 2, S - 1)
                if c_c >= 1:
                    rank(c_c - 1)
                if 0 <= c_b < NC:
                    att_out(c_b)
                if c_a + 1 < NC:
                    x0_transposes(c_a + 1)
                if c_a + 1 < NC:
                    for s in range(3):
                        project(c_a + 1, s)
                if tick == NC - 1:
                    shared_up(0, 0)
                if tick == NC:
                    shared_down(0)
                    shared_up(1, 0)
                if tick == NC + 1:
                    shared_up(2, 0)
                    shared_down(1)
                    shared_up(2, 1)
                if c_c >= 0:
                    x2_transposes(c_c)
                if c_a + 1 < NC:
                    project(c_a + 1, 3)
                if tick == NC:
                    x1_transposes(c_b)
                if tick == NC + 1:
                    shared_down(2)
                if c_c >= 0:
                    logits(c_c)
                if 0 <= c_b < NC:
                    if tick < NC:
                        x1_transposes(c_b)
                    features(c_b)
                if tick == NC - 1:
                    shared_up(0, 1)
                if tick == NC:
                    shared_up(1, 1)
            shared_up(3, 0)
            rank(NC - 1)
            shared_up(3, 1)
            pe.wait_ge(pos_sb, NC)
            pe.matmul(bank[7][:, 0:E], ones16[:], cum[:, NC * S * E:(NC * S + 1) * E], start=True, stop=True
                      ).then_inc(cnt_ps, 1)
            shared_down(3)

            def turn(b, q, r, nth, reuse=True):
                pe.wait_ge(ld_slot[r], 16 * nth + 16)
                if reuse:
                    pe.wait_ge(xst_sb, b - 1)
                pe.transpose(bank[q][:, 0:D], slots[:, r * RW:r * RW + D], ident[:]).then_inc(xst_ps, 1)

            def experts_of(b, n):
                return nc.values_load_multi_w_load_instructions(
                    blk_e[0:1, ds(b, n)], engines=[mybir.EngineType.PE], min_val=0, max_val=E - 1,
                    skip_runtime_bounds_check_because="experts worked out on the chip, at most E - 1")[1]

            def up(b, q, ex, reuse=True):
                pe.wait_ge(xst_sb, b + 1)
                if reuse:
                    pe.wait_ge(ac_sb, b - 1)
                pe.matmul(bank[2 + q][:], xs_t[:, q * D:(q + 1) * D], rt_gu[:, ds(ex * (2 * I), 2 * I)],
                          start=True, stop=True).then_inc(gu_ps, 1)

            def turn_hidden(b, q, reuse=True):
                pe.wait_ge(ac_sb, b + 1)
                if reuse:
                    pe.wait_ge(act_sb, b - 1)
                for h in range(HALVES):
                    last = pe.transpose(bank[4 + q][:, h * P:(h + 1) * P], ac[:, q * I + h * P:q * I + (h + 1) * P], ident[:])
                last.then_inc(act_ps, 1)

            def down(b, q, ex, reuse=True):
                pe.wait_ge(act_sb, b + 1)
                if reuse:
                    pe.wait_ge(r3_sb, b - 1)
                for h in range(HALVES):
                    last = pe.matmul(bank[6 + q][:, 0:D], ac_t[:, q * I + h * P:q * I + (h + 1) * P],
                                     rt_dn[:, ds(ex * (HALVES * D) + h * D, D)], start=h == 0, stop=h == HALVES - 1)
                last.then_inc(y_ps, 1)

            pe.wait_ge(ld_rt, 48)
            pe.wait_ge(tab, TAB + 1)
            pe.wait_ge(rowb_sb, 2 * NC)
            def step(b, r, nth, ex, reuse=True):
                turn(b + 1, (r + 1) % 2, (r + 1) % RING, nth)
                up(b, r % 2, ex[1])
                turn_hidden(b - 1, (r + 1) % 2, reuse)
                down(b - 2, r % 2, ex[0], reuse)

            FIRST = 4
            ex = experts_of(0, FIRST)
            turn(0, 0, 0, 0, False)
            turn(1, 1, 1, 0, False)
            up(0, 0, ex[0], False)
            turn(2, 0, 2, 0)
            up(1, 1, ex[1], False)
            turn_hidden(0, 0, False)
            step(2, 2, 0, [ex[0], ex[2]], False)
            step(3, 3, 0, [ex[1], ex[3]], False)
            with pe.Fori(0, (NB - 5) // RING) as k:
                ex = experts_of(RING * k + FIRST - 2, RING + 2)
                for n in range(RING):
                    r = (FIRST + n) % RING
                    nth = k + (FIRST + n + 1) // RING
                    step(RING * k + (FIRST + n), r, nth, [ex[n], ex[n + 2]])
            ex = experts_of(NB - 3, 3)
            up(NB - 1, (NB - 1) % 2, ex[2])
            turn_hidden(NB - 2, (NB - 2) % 2)
            down(NB - 3, (NB - 3) % 2, ex[0])
            turn_hidden(NB - 1, (NB - 1) % 2)
            down(NB - 2, (NB - 2) % 2, ex[1])
            down(NB - 1, (NB - 1) % 2, ex[2])


_INS = ["x", "ctx_1024", "L0_attn_Wq", "L0_attn_bq", "L0_attn_Wk", "L0_attn_bk", "L0_attn_Wv", "L0_attn_bv",
        "L0_attn_Wo", "L0_attn_bo", "L0_attn_beta", "L0_xattn_projection", "L0_ffn_gate_w", "L0_ffn_sh_gate",
        "L0_ffn_sh_up", "L0_ffn_sh_down", "L0_ffn_rt_gate", "L0_ffn_rt_up", "L0_ffn_rt_down"]


def kernel(**inputs):
    import concourse.bacc as bacc
    from concourse.bass_utils import run_bass_kernel_spmd

    nc = bacc.Bacc("TRN2", target_bir_lowering=False, num_devices=1)
    arrays, t = {}, {}
    for name in _INS:
        a = np.ascontiguousarray(inputs[name])
        arrays[f"in_{name}"] = a
        t[name] = nc.dram_tensor(f"in_{name}", a.shape, mybir.dt.from_np(a.dtype), kind="ExternalInput").ap()
    t["out"] = nc.dram_tensor("out_x", inputs["x"].shape, mybir.dt.float32, kind="ExternalOutput").ap()
    build_decoder(nc, t)
    r = run_bass_kernel_spmd(nc, [arrays], core_ids=[0])
    return r.results[0]["out_x"]
```

```python
import math
from contextlib import ExitStack

import numpy as np

import concourse.bass as bass
from concourse import mybir


def build_decoder(nc, t):
    F32 = mybir.dt.float32
    BF16 = mybir.dt.bfloat16
    I32 = mybir.dt.int32
    ALU = mybir.AluOpType
    ACT = mybir.ActivationFunctionType
    X = mybir.AxisListType.X
    ds = bass.ds

    P = 128
    S, BATCH, D = t["x"].shape
    NC = BATCH // P
    TOK = S * BATCH
    HEADS, DH = 16, D // 16
    CTX = t["ctx_1024"].shape[1]
    M = t["L0_xattn_projection"].shape[0]
    E, _, I = t["L0_ffn_rt_gate"].shape
    HALVES = I // P
    PAIRS = S * (S + 1) // 2 - 1
    PB = [0, 0, 2, 5]
    EPS_LN, EPS_X = 1e-5, 1e-6
    INV_SQRT_D = 1.0 / math.sqrt(D)
    INV_SQRT_DH = 1.0 / math.sqrt(DH)
    NB = TOK // P + E - 1
    ROWS = TOK + P
    FILLER = E * ROWS
    AT_SCORE, AT_BASE, AT_TOKEN = D, D + 1, 2 * D + 1
    RW = 2 * D + 2
    NOTOK = 1 << 20
    KB = TOK // P
    RING = 6
    NBP = -(-NB // RING) * RING

    x_in = t["x"].rearrange("s (c p) d -> c p s d", p=P)
    out_rows = t["out"].rearrange("s b d -> (s b) d")

    ctx = ExitStack()
    with ctx:
        def sb(name, shape, dt=F32):
            return ctx.enter_context(nc.sbuf_tensor(name, shape, dt))

        def sem(name):
            return ctx.enter_context(nc.semaphore(name))

        table = nc.dram_tensor("slot_table", (FILLER + P, RW), F32, kind="Internal").ap()

        ident = sb("ident", [P, P])
        before = sb("before", [P, P], BF16)
        ones16 = sb("ones16", [P, P], BF16)
        rev = sb("rev", [P, E])
        region = sb("region", [P, E])
        kcol = sb("kcol", [1, KB])
        bcol = sb("bcol", [1, NBP])
        upto = sb("upto", [1, E * E])
        spread = sb("spread", [65, P], BF16)
        bias3 = sb("bias3", [65, 4 * P], BF16)
        brest = sb("brest", [65, 4 * P])
        mhalf = sb("mhalf", [P, S])
        filler = sb("filler", [P, RW])
        w_nat = sb("w_nat", [P, 4 * P])
        w_t = sb("w_t", [P, 4 * P])
        bias = sb("bias", [P, 4 * P])
        beta = sb("beta", [P, HEADS])
        silu_warm = sb("silu_warm", [1, 1])
        qscale = sb("qscale", [P, HEADS])
        proj = sb("proj", [M, D])
        proj_t = sb("proj_t", [D, M])
        ctx1 = sb("ctx1", [CTX, S * (D + 1)])
        ctx_t = sb("ctx_t", [D, S * CTX])
        rf_k = sb("rf_k", [CTX, S * M])
        kvz = sb("kvz", [M, S * (D + 1)])
        gate = sb("gate", [D, E])
        sh_gu = sb("sh_gu", [D, 2 * I])
        sh_dn = sb("sh_dn", [P, HALVES * D])
        rt_gu = sb("rt_gu", [D, E * 2 * I])
        rt_dn = sb("rt_dn", [P, E * HALVES * D])

        CW = S * D
        x0 = sb("x0", [P, NC * CW])
        x0_t = sb("x0_t", [P, NC * CW])
        qkv = sb("qkv", [P, NC * S * 3 * D])
        pq = sb("pq", [P, PAIRS * D])
        SW = (S - 1) * S * HEADS
        score = sb("score", [P, NC * SW])
        smax = sb("smax", [P, NC * (S - 1) * HEADS])
        ssub = sb("ssub", [P, NC * SW])
        prob = sb("prob", [P, NC * SW])
        ssum = sb("ssum", [P, NC * (S - 1) * HEADS])
        srec = sb("srec", [P, NC * (S - 1) * HEADS])
        pv = sb("pv", [P, PAIRS * D])
        att_t = sb("att_t", [P, CW])
        r2 = sb("r2", [P, CW])
        st = sb("st", [P, NC * 2 * S * 6])
        mv = sb("mv", [P, NC * 2 * S * 2])
        ve = sb("ve", [P, NC * 2 * S])
        rs = sb("rs", [P, NC * 2 * S])
        x1 = sb("x1", [P, NC * CW])
        x1_t = sb("x1_t", [P, CW])
        rf_q = sb("rf_q", [M, CW])
        den = sb("den", [P, NC * S])
        rden = sb("rden", [P, NC * S])
        rows = sb("rows", [P, NC * S * RW])
        x2_t = sb("x2_t", [P, NC * CW])
        sg = sb("sg", [P, HALVES * CW])
        hid = sb("hid", [P, 2 * HALVES * CW])
        ltop = sb("ltop", [P, NC * S])
        leq = sb("leq", [P, NC * S * E])
        lcand = sb("lcand", [P, NC * S * E])
        lfirst = sb("lfirst", [P, NC * S])
        hot = sb("hot", [P, NC * S * E], BF16)
        cum = sb("cum", [P, NC * E], BF16)
        tsc = sb("tsc", [P, NC * S])
        rk = sb("rk", [P, NC * S * E])
        rkh = sb("rkh", [P, NC * S * E])
        pos = sb("pos", [P, NC * S], I32)

        cnt = sb("cnt", [1, E])
        gtk = sb("gtk", [1, E * KB])
        nblk = sb("nblk", [1, E])
        nmask = sb("nmask", [1, E * E])
        cblk = sb("cblk", [1, E])
        dstep = sb("dstep", [1, E])
        ge = sb("ge", [1, NBP * E])
        ged = sb("ged", [1, NBP * E])
        esum = sb("esum", [1, NBP])
        rsum = sb("rsum", [1, NBP])
        radd = sb("radd", [1, NBP])
        blk_e = sb("blk_e", [1, NBP], I32)
        blk_row = sb("blk_row", [1, NBP], I32)
        tail_row = sb("tail_row", [1, E], I32)

        slots = sb("slots", [P, RING * RW])
        token = sb("token", [P, RING], I32)
        xs_t = sb("xs_t", [P, 2 * D])
        si = sb("si", [P, 2 * I])
        ac = sb("ac", [P, 2 * I])
        ac_t = sb("ac_t", [P, 2 * I])
        r3 = sb("r3", [P, RING * D])
        st3 = sb("st3", [P, RING * 6])
        mv3 = sb("mv3", [P, RING * 2])
        ve3 = sb("ve3", [P, RING])
        rs3 = sb("rs3", [P, RING])
        fin = sb("fin", [P, RING * D])

        bank = [ctx.enter_context(nc.psum_tensor(f"bank{i}", [P, 512], F32)) for i in range(8)]

        ld_w, ld_bias, ld_beta, ld_ctx, ld_proj, ld_gate = map(
            sem, ["ld_w", "ld_bias", "ld_beta", "ld_ctx", "ld_proj", "ld_gate"])
        ld_x = [sem(f"ld_x{c}") for c in range(NC)]
        ld_sh, ld_rt = sem("ld_sh"), sem("ld_rt")
        k_zero, k_mask, k_spread, k_const = sem("k_zero"), sem("k_mask"), sem("k_spread"), sem("k_const")
        w_ps, w_sb, qs_sb, b3_sb, c_ps, c_sb, fk_ps, fk_sb, kv_ps, kv_sb = map(
            sem, ["w_ps", "w_sb", "qs_sb", "b3_sb", "c_ps", "c_sb", "fk_ps", "fk_sb", "kv_ps", "kv_sb"])
        x0t_ps, x0t_sb, qkv_ps, qkv_sb, pq_sb = map(
            sem, ["x0t_ps", "x0t_sb", "qkv_ps", "qkv_sb", "pq_sb"])
        score_sb, smax_sb, ssub_sb, exp_sb, ssum_sb, srec_sb, prob_sb, pv_sb = map(
            sem, ["score_sb", "smax_sb", "ssub_sb", "exp_sb", "ssum_sb", "srec_sb", "prob_sb", "pv_sb"])
        att_ps, att_t_sb, ao_ps = map(sem, ["att_ps", "att_t_sb", "ao_ps"])
        st1_sb, mv1_sb, ve1_sb, rs1_sb, x1_sb = map(
            sem, ["st1_sb", "mv1_sb", "ve1_sb", "rs1_sb", "x1_sb"])
        x1t_ps, x1t_sb, fq_ps, fq_sb, xo_ps, den_sb, rden_sb = map(
            sem, ["x1t_ps", "x1t_sb", "fq_ps", "fq_sb", "xo_ps", "den_sb", "rden_sb"])
        r2_sb, st2_sb, mv2_sb, ve2_sb, rs2_sb, x2_sb, x2t_ps, x2t_sb = map(
            sem, ["r2_sb", "st2_sb", "mv2_sb", "ve2_sb", "rs2_sb", "x2_sb", "x2t_ps", "x2t_sb"])
        lg_ps, ltop_sb, leq_sb, lcand_sb, lfirst_sb, hot_sb, cum_sb, tsc_sb, sc_sb, rank_ps, rk_sb, rkh_sb, pos_sb = map(
            sem, ["lg_ps", "ltop_sb", "leq_sb", "lcand_sb", "lfirst_sb", "hot_sb", "cum_sb", "tsc_sb", "sc_sb",
                  "rank_ps", "rk_sb", "rkh_sb", "pos_sb"])
        scat, fill = sem("scat"), sem("fill")
        g_ps, sg_sb, gated_sb, hid_sb, sy_ps, rowb_sb = map(
            sem, ["g_ps", "sg_sb", "gated_sb", "hid_sb", "sy_ps", "rowb_sb"])
        cnt_ps, tab = sem("cnt_ps"), sem("tab")
        ld_slot = [sem(f"ld_slot{q}") for q in range(RING)]
        xst_ps, xst_sb, gu_ps, si_sb, ac_sb, act_ps, act_sb, y_ps = map(
            sem, ["xst_ps", "xst_sb", "gu_ps", "si_sb", "ac_sb", "act_ps", "act_sb", "y_ps"])
        r3_sb, st3_sb, mv3_sb, ve3_sb, rs3_sb, fin_sb = map(
            sem, ["r3_sb", "st3_sb", "mv3_sb", "ve3_sb", "rs3_sb", "fin_sb"])
        out_dma = [sem(f"out_dma{q}") for q in range(RING)]

        TAB_TAILS, TAB = 2, 13

        def tile_of(buf, c, s, w=D, row=None):
            row = w if row is None else row
            return buf[:, ds((c * S + s) * row, w)]

        def chunk_of(buf, c, w):
            return buf[:, ds(c * w, w)]

        def rows_part(c, at, w):
            return rows[:, c * S * RW:(c + 1) * S * RW].rearrange("p (s w) -> p s w", s=S)[:, :, at:at + w]

        def qkv_part(c, s, part, n=1):
            v = qkv[:, ds((c * S + s) * 3 * D, n * 3 * D)].rearrange("p (j w) -> p j w", w=3 * D)
            return v[:, :, part * D:(part + 1) * D]

        def shared_banks(c, h):
            return (0, 3) if c and h else (1, 2)

        SHARED_OUT = [0, 4, 5, 4]

        def pair_products(engine, c, i):
            return engine.tensor_tensor(pq[:, PB[i] * D:(PB[i] + i + 1) * D].rearrange("p (j d) -> p j d", d=D),
                                        qkv_part(c, 0, 1, i + 1), qkv_part(c, i, 0).to_broadcast([P, i + 1, D]), ALU.mult)

        block = ctx.enter_context(nc.Block())

        @block.sync
        def _(sp):
            sp.dma_start(x0[:, 0:CW].rearrange("p (s d) -> p s d", s=S), x_in[0]).then_inc(ld_x[0], 16)
            for n, w in enumerate(("bq", "bk", "bv", "bo")):
                sp.dma_start(bias[:, n * D:(n + 1) * D], t[f"L0_attn_{w}"].unsqueeze(0).to_broadcast([P, D])).then_inc(ld_bias, 16)
            for n, w in ((2, "Wv"), (3, "Wo")):
                sp.dma_start(w_nat[:, n * P:(n + 1) * P], t[f"L0_attn_{w}"]).then_inc(ld_w, 16)
            sp.dma_start(ctx1[:].rearrange("p (s w) -> p s w", s=S)[:, :, 0:D],
                         t["ctx_1024"].rearrange("s l d -> l s d")).then_inc(ld_ctx, 16)
            sp.dma_start(proj[:], t["L0_xattn_projection"]).then_inc(ld_proj, 16)
            for c in range(1, NC):
                sp.dma_start(x0[:, c * CW:(c + 1) * CW].rearrange("p (s d) -> p s d", s=S), x_in[c]).then_inc(ld_x[c], 16)
            sp.dma_start(gate[:], t["L0_ffn_gate_w"]).then_inc(ld_gate, 16)
            sp.dma_start(sh_gu[:, 0:I], t["L0_ffn_sh_gate"]).then_inc(ld_sh, 16)
            sp.dma_start(sh_gu[:, I:2 * I], t["L0_ffn_sh_up"]).then_inc(ld_sh, 16)
            sp.dma_start(sh_dn[:].rearrange("p (h d) -> p h d", h=HALVES),
                         t["L0_ffn_sh_down"].rearrange("(h p) d -> p h d", p=P)).then_inc(ld_sh, 16)
            gu = rt_gu[:].rearrange("p (e i) -> p e i", e=E)
            sp.dma_start(gu[:, :, 0:I], t["L0_ffn_rt_gate"].rearrange("e h i -> h e i")).then_inc(ld_rt, 16)
            sp.dma_start(gu[:, :, I:2 * I], t["L0_ffn_rt_up"].rearrange("e h i -> h e i")).then_inc(ld_rt, 16)
            sp.dma_start(rt_dn[:].rearrange("p (e h d) -> p e h d", e=E, h=HALVES),
                         t["L0_ffn_rt_down"].rearrange("e (h p) d -> p e h d", p=P)).then_inc(ld_rt, 16)
            sp.wait_ge(k_const, 1)
            sp.dma_start(table[FILLER:FILLER + P, :], filler[:]).then_inc(fill, 16)

            sp.wait_ge(tab, TAB_TAILS)
            tails = nc.values_load_multi_w_load_instructions(
                tail_row[0:1, :], engines=[mybir.EngineType.SP], min_val=0, max_val=FILLER - P,
                skip_runtime_bounds_check_because="rows worked out on the chip, inside the expert's region")[1]
            for row in tails:
                sp.dma_start(table[ds(row, P), :], filler[:]).then_inc(fill, 16)

            def round_of(b):
                return nc.values_load_multi_w_load_instructions(
                    blk_row[0:1, ds(b, RING)], engines=[mybir.EngineType.SP], min_val=0, max_val=FILLER,
                    skip_runtime_bounds_check_because="rows worked out on the chip, at most FILLER")[1]

            def load(row, q, used=None):
                if used is not None:
                    sp.wait_ge(r3_sb, used)
                sp.dma_start(slots[:, q * RW:(q + 1) * RW], table[ds(row, P), :]).then_inc(ld_slot[q], 16)

            sp.wait_ge(tab, TAB)
            first = round_of(0)
            sp.wait_ge(scat, 16 * NC * S)
            sp.wait_ge(fill, 16 * (E + 1))
            for q in range(RING):
                load(first[q], q)
            with sp.Fori(0, NBP // RING - 1) as k:
                after = round_of(RING * k + RING)
                for q in range(RING):
                    load(after[q], q, RING * k + q + 1)
            for q in range(RING):
                sp.wait_ge(ld_slot[q], 16 * (NBP // RING))
                sp.wait_ge(out_dma[q], 16 * ((NB - 1 - q) // RING + 1))

        @block.gpsimd
        def _(g):
            g.memset(ident[:], 0.0).then_inc(k_zero, 1)
            g.memset(ones16[:], 1.0).then_inc(k_zero, 1)
            g.wait_ge(k_zero, 2)
            g.affine_select(out=ident[:], in_=ident[:], compare_op=ALU.not_equal, fill=1.0, base=0,
                            pattern=[[-1, P]], channel_multiplier=1).then_inc(k_mask, 1)
            g.affine_select(out=before[:], in_=ones16[:], compare_op=ALU.is_gt, fill=0.0, base=0,
                            pattern=[[1, P]], channel_multiplier=-1).then_inc(k_mask, 1)
            g.memset(ctx1[:].rearrange("p (s w) -> p s w", s=S)[:, :, D:D + 1], 1.0)
            g.memset(score[:], -1e30)
            g.memset(upto[:], 1.0)
            g.memset(filler[:, 0:AT_TOKEN], 0.0)
            g.memset(filler[:, AT_TOKEN:RW].bitcast(I32), NOTOK)
            g.memset(mhalf[:], -0.5)
            g.memset(cum[:, 0:E], 0.0)
            for c in range(NC):
                col = rows_part(c, AT_TOKEN, 1)
                g.iota(col.bitcast(I32), pattern=[[BATCH, S], [1, 1]], base=c * P, channel_multiplier=1)
            g.iota(rev[:], pattern=[[-1, E]], base=E, channel_multiplier=0, allow_small_or_imprecise_dtypes=True)
            g.iota(region[:], pattern=[[ROWS, E]], base=0, channel_multiplier=0, allow_small_or_imprecise_dtypes=True)
            g.iota(kcol[:], pattern=[[P, KB]], base=0, channel_multiplier=0, allow_small_or_imprecise_dtypes=True)
            g.iota(bcol[:], pattern=[[1, NBP]], base=0, channel_multiplier=0, allow_small_or_imprecise_dtypes=True
                   ).then_inc(k_const, 1)
            g.wait_ge(k_const, 1)
            g.affine_select(out=upto[:], in_=upto[:], compare_op=ALU.is_ge, fill=0.0, base=0,
                            pattern=[[1, E], [-1, E]], channel_multiplier=0).then_inc(k_const, 1)

            def products(c):
                if c:
                    g.wait_ge(score_sb, 3 * c)
                for i in range(1, S):
                    g.wait_ge(qkv_sb, S * c + i + 1)
                    pair_products(g, c, i).then_inc(pq_sb, 1)

            def rstd(n, c, mv_ready, ve_done, rs_done):
                g.wait_ge(mv_ready, S * c + S)
                at = (c * 2 + n) * S
                var = mv[:, at * 2:(at + S) * 2].rearrange("p (s w) -> p s w", w=2)[:, :, 1:2]
                g.tensor_scalar(ve[:, at:at + S], var, EPS_LN, None, ALU.add).then_inc(ve_done, 1)
                g.wait_ge(ve_done, c + 1)
                g.tensor_tensor(rs[:, at:at + S], ve[:, at:at + S], mhalf[:], ALU.pow).then_inc(rs_done, 1)

            def rstd1(c):
                rstd(0, c, mv1_sb, ve1_sb, rs1_sb)

            def rstd2(c):
                rstd(1, c, mv2_sb, ve2_sb, rs2_sb)

            def count(c):
                g.wait_ge(hot_sb, c + 1)
                for s in range(S):
                    if c or s:
                        g.wait_ge(cum_sb, S * c + s)
                    before_tile = cum[:, (c + 1) * E:(c + 2) * E] if s else cum[:, c * E:(c + 1) * E]
                    g.tensor_tensor(cum[:, (c + 1) * E:(c + 2) * E], before_tile,
                                    hot[:, (c * S + s) * E:(c * S + s + 1) * E], ALU.add).then_inc(cum_sb, 1)

            def score_of(c):
                g.wait_ge(tsc_sb, c + 1)
                g.tensor_scalar(rows_part(c, AT_SCORE, 1), chunk_of(tsc, c, S).unsqueeze(2), 0.5, 0.5, ALU.mult, ALU.add).then_inc(sc_sb, 1)

            def scatter(c):
                g.wait_ge(pos_sb, c + 1)
                g.wait_ge(sc_sb, c + 1)
                for s in range(S):
                    if s % 2 == 0:
                        g.wait_ge(rowb_sb, 2 * c + s // 2 + 1)
                    g.indirect_dma_start(
                        out=table[:, :],
                        out_offset=bass.IndirectOffsetOnAxis(ap=pos[:, c * S + s:c * S + s + 1], axis=0),
                        in_=tile_of(rows, c, s, RW), in_offset=None).then_inc(scat, 16)

            products(0)
            products(1)
            rstd1(0)
            products(2)
            rstd2(0)
            rstd1(1)
            count(0)
            products(3)
            rstd2(1)
            rstd1(2)
            count(1)
            rstd2(2)
            rstd1(3)
            score_of(0)
            score_of(1)
            count(2)
            scatter(0)
            rstd2(3)
            scatter(1)
            score_of(2)
            scatter(2)
            score_of(3)
            scatter(3)

            def rstd3(b, r):
                g.wait_ge(ve3_sb, b + 1)
                g.tensor_tensor(rs3[:, r:r + 1], ve3[:, r:r + 1], mhalf[:, 0:1], ALU.pow).then_inc(rs3_sb, 1)

            last_token = g.to_reg(TOK - 1)

            def send(r):
                g.indirect_dma_start(
                    out=out_rows, out_offset=bass.IndirectOffsetOnAxis(ap=token[:, r:r + 1], axis=0),
                    in_=fin[:, r * D:(r + 1) * D], in_offset=None,
                    bounds_check=last_token, oob_is_err=False).then_inc(out_dma[r], 16)

            rstd3(0, 0)
            with g.Fori(0, (NB - 5) // RING) as k:
                for r in range(RING):
                    rstd3(RING * k + r + 1, (r + 1) % RING)
                    send(r)
            for b in range(NB - 5, NB):
                if b + 1 < NB:
                    rstd3(b + 1, (b + 1) % RING)
                g.wait_ge(fin_sb, b + 1)
                send(b % RING)

        @block.scalar
        def _(a):
            a.dma_start(beta[:], t["L0_attn_beta"].unsqueeze(0).to_broadcast([P, HEADS])).then_inc(ld_beta, 16)
            for n, w in ((0, "Wq"), (1, "Wk")):
                a.dma_start(w_nat[:, n * P:(n + 1) * P], t[f"L0_attn_{w}"]).then_inc(ld_w, 16)
            a.wait_ge(ld_beta, 16)
            a.activation(qscale[:], beta[:], ACT.Exp, scale=-1.0).then_inc(qs_sb, 1)

            def weight_copy():
                a.wait_ge(w_ps, 1)
                a.copy(w_t[:, D:4 * D], bank[3][:, D:4 * D]).then_inc(w_sb, 1)

            def copy_x0t(c):
                a.wait_ge(x0t_ps, c + 1)
                a.copy(chunk_of(x0_t, c, CW), bank[0][:]).then_inc(x0t_sb, 1)

            def copy_qkv(c, s):
                a.wait_ge(qkv_ps, S * c + s + 1)
                a.copy(qkv[:, (c * S + s) * 3 * D:(c * S + s + 1) * 3 * D], bank[1 + s % 2][:, 0:3 * D]).then_inc(qkv_sb, 1)

            def exps(c):
                a.wait_ge(ssub_sb, c + 1)
                a.activation(chunk_of(prob, c, SW), chunk_of(ssub, c, SW), ACT.Exp).then_inc(exp_sb, 1)

            def copy_att(c):
                a.wait_ge(att_ps, c + 1)
                if c:
                    a.wait_ge(ao_ps, c)
                a.copy(att_t[:], bank[0][:]).then_inc(att_t_sb, 1)

            def copy_x1t(c):
                a.wait_ge(x1t_ps, c + 1)
                a.copy(x1_t[:], bank[4][:]).then_inc(x1t_sb, 1)

            def features_q(c):
                a.wait_ge(fq_ps, c + 1)
                if c:
                    a.wait_ge(xo_ps, c)
                a.activation(rf_q[:], bank[4][0:M, :], ACT.Exp, scale=INV_SQRT_D).then_inc(fq_sb, 1)

            def copy_x2t(c):
                a.wait_ge(x2t_ps, c + 1)
                a.copy(chunk_of(x2_t, c, CW), bank[7][:]).then_inc(x2t_sb, 1)

            def score_tanh(c):
                a.wait_ge(ltop_sb, c + 1)
                a.activation(chunk_of(tsc, c, S), chunk_of(ltop, c, S), ACT.Tanh, scale=0.5).then_inc(tsc_sb, 1)

            def shared_tanh(c, h):
                a.wait_ge(g_ps, 2 * c + h + 1)
                a.activation(sg[:, h * CW:(h + 1) * CW], bank[shared_banks(c, h)[0]][:], ACT.Tanh, scale=0.5
                             ).then_inc(sg_sb, 1)

            def context_exp():
                a.wait_ge(fk_ps, 1)
                a.activation(rf_k[:], bank[6][0:CTX, 0:S * M], ACT.Exp, scale=INV_SQRT_D).then_inc(fk_sb, 1)

            copy_x0t(0)
            weight_copy()
            copy_qkv(0, 0)
            copy_qkv(0, 1)
            copy_qkv(0, 2)
            copy_qkv(0, 3)
            context_exp()
            copy_x0t(1)
            exps(0)
            copy_qkv(1, 0)
            copy_qkv(1, 1)
            copy_qkv(1, 2)
            copy_att(0)
            copy_qkv(1, 3)
            copy_x0t(2)
            exps(1)
            copy_qkv(2, 0)
            copy_qkv(2, 1)
            copy_qkv(2, 2)
            copy_x1t(0)
            features_q(0)
            copy_qkv(2, 3)
            copy_att(1)
            copy_x0t(3)
            exps(2)
            copy_qkv(3, 0)
            copy_qkv(3, 1)
            copy_x2t(0)
            copy_x1t(1)
            copy_qkv(3, 2)
            features_q(1)
            copy_qkv(3, 3)
            score_tanh(0)
            copy_att(2)
            shared_tanh(0, 0)
            copy_x2t(1)
            exps(3)
            copy_x1t(2)
            shared_tanh(0, 1)
            features_q(2)
            score_tanh(1)
            copy_att(3)
            copy_x2t(2)
            shared_tanh(1, 0)
            copy_x1t(3)
            features_q(3)
            shared_tanh(1, 1)
            shared_tanh(2, 0)
            score_tanh(2)
            shared_tanh(2, 1)
            copy_x2t(3)
            shared_tanh(3, 0)
            shared_tanh(3, 1)
            score_tanh(3)

            a.activation(silu_warm[:], qscale[0:1, 0:1], ACT.Silu)

            def copy_xst(b, q):
                a.wait_ge(xst_ps, b + 1)
                a.copy(xs_t[:, q * D:(q + 1) * D], bank[q][:, 0:D]).then_inc(xst_sb, 1)

            def silu(b, q, r):
                a.wait_ge(gu_ps, b + 1)
                a.activation(si[:, q * I:(q + 1) * I], bank[2 + q][:, 0:I], ACT.Silu,
                             scale=slots[:, r * RW + AT_SCORE:r * RW + AT_SCORE + 1]).then_inc(si_sb, 1)

            def copy_act(b, q):
                a.wait_ge(act_ps, b + 1)
                a.copy(ac_t[:, q * I:(q + 1) * I], bank[4 + q][:, 0:I]).then_inc(act_sb, 1)

            def step(b, r, more=2):
                if more > 1:
                    copy_xst(b + 2, r % 2)
                if more > 0:
                    silu(b + 1, (r + 1) % 2, (r + 1) % RING)
                copy_act(b, r % 2)

            copy_xst(0, 0)
            copy_xst(1, 1)
            silu(0, 0, 0)
            with a.Fori(0, (NB - 5) // RING) as k:
                for r in range(RING):
                    step(RING * k + r, r)
            for b in range(NB - 5, NB):
                step(b, b % RING, NB - 1 - b)

        @block.vector
        def _(v):
            v.wait_ge(k_const, 1)
            v.memset(spread[:], 0.0).then_inc(k_spread, 1)
            v.wait_ge(k_spread, 1)
            for part in range(3):
                v.memset(spread[32 * part:32 * part + 1, :], 1.0).then_inc(k_spread, 1)
            scale_b = qscale[:].unsqueeze(2).to_broadcast([P, HEADS, DH])
            heads = lambda ap: ap.rearrange("p (h d) -> p h d", h=HEADS)
            v.wait_ge(ld_bias, 64)
            v.wait_ge(qs_sb, 1)
            v.scalar_tensor_tensor(heads(bias[:, 0:D]), heads(bias[:, 0:D]), INV_SQRT_DH, scale_b,
                                   ALU.mult, ALU.mult).then_inc(b3_sb, 1)
            with nc.allow_low_precision(reason="the three parts add up to the float32 bias"):
                v.wait_ge(b3_sb, 1)
                v.tensor_copy(bias3[:], bias[0:65, :]).then_inc(b3_sb, 1)
                v.wait_ge(b3_sb, 2)
                v.tensor_tensor(brest[:], bias[0:65, :], bias3[:], ALU.subtract).then_inc(b3_sb, 1)
                v.wait_ge(b3_sb, 3)
                v.tensor_copy(bias3[32:33, :], brest[32:33, :]).then_inc(b3_sb, 1)
                v.tensor_copy(bias3[64:65, :], brest[64:65, :]).then_inc(b3_sb, 1)
            v.wait_ge(w_ps, 1)
            v.scalar_tensor_tensor(heads(w_t[:, 0:D]), heads(bank[4][:, 0:D]), INV_SQRT_DH, scale_b,
                                   ALU.mult, ALU.mult).then_inc(w_sb, 1)
            with nc.allow_low_precision(reason="the three parts add up to the float32 bias"):
                v.wait_ge(b3_sb, 5)
                v.tensor_tensor(bias3[64:65, :], brest[64:65, :], bias3[64:65, :], ALU.subtract).then_inc(b3_sb, 1)

            def scores(c, i):
                v.wait_ge(pq_sb, 3 * c + i)
                at = c * SW + (i - 1) * S * HEADS
                v.tensor_reduce(score[:, at:at + (i + 1) * HEADS],
                                pq[:, PB[i] * D:(PB[i] + i + 1) * D].rearrange("p (g d) -> p g d", d=DH),
                                X, ALU.add).then_inc(score_sb, 1)

            def by_query(ap):
                return ap.rearrange("p (i j h) -> p i h j", i=S - 1, j=S)

            SQ = (S - 1) * HEADS

            def over_keys(ap):
                return ap.rearrange("p (i h) -> p i h", i=S - 1).unsqueeze(3).to_broadcast([P, S - 1, HEADS, S])

            def softmax_max(c):
                v.wait_ge(score_sb, 3 * c + 3)
                v.tensor_reduce(chunk_of(smax, c, SQ), by_query(chunk_of(score, c, SW)), X, ALU.max).then_inc(smax_sb, 1)

            def softmax_sub(c):
                v.wait_ge(smax_sb, c + 1)
                v.tensor_tensor(by_query(chunk_of(ssub, c, SW)), by_query(chunk_of(score, c, SW)),
                                over_keys(chunk_of(smax, c, SQ)), ALU.subtract).then_inc(ssub_sb, 1)

            def softmax_sum(c):
                v.wait_ge(exp_sb, c + 1)
                v.tensor_reduce(chunk_of(ssum, c, SQ), by_query(chunk_of(prob, c, SW)), X, ALU.add).then_inc(ssum_sb, 1)

            def softmax_reciprocal(c):
                v.wait_ge(ssum_sb, c + 1)
                v.reciprocal(chunk_of(srec, c, SQ), chunk_of(ssum, c, SQ)).then_inc(srec_sb, 1)

            def softmax_scale(c):
                v.wait_ge(srec_sb, c + 1)
                v.tensor_tensor(by_query(chunk_of(prob, c, SW)), by_query(chunk_of(prob, c, SW)),
                                over_keys(chunk_of(srec, c, SQ)), ALU.mult).then_inc(prob_sb, 1)

            def attend(c, i):
                v.wait_ge(prob_sb, c + 1)
                if c:
                    v.wait_ge(att_ps, c)
                n = (i + 1) * HEADS
                at = c * SW + (i - 1) * S * HEADS
                p = prob[:, at:at + n].rearrange("p (j h) -> p j h", h=HEADS)
                v.tensor_tensor(
                    pv[:, PB[i] * D:(PB[i] + i + 1) * D].rearrange("p (j h d) -> p j h d", h=HEADS, d=DH),
                    qkv_part(c, 0, 2, i + 1).rearrange("p j (h d) -> p j h d", d=DH),
                    p.unsqueeze(3).to_broadcast([P, i + 1, HEADS, DH]), ALU.mult).then_inc(pv_sb, 1)

            def stats(n, c, src, st_done):
                for s in range(S):
                    at = (c * 2 + n) * S + s
                    v.bn_stats(st[:, at * 6:(at + 1) * 6], src[:, s * D:(s + 1) * D]).then_inc(st_done, 1)

            def moments(n, c, st_done, mv_done):
                for s in range(S):
                    at = (c * 2 + n) * S + s
                    v.wait_ge(st_done, S * c + s + 1)
                    v.bn_aggr(mv[:, at * 2:(at + 1) * 2], st[:, at * 6:(at + 1) * 6]).then_inc(mv_done, 1)

            def stats1(c):
                v.wait_ge(ao_ps, c + 1)
                stats(0, c, bank[3], st1_sb)

            def moments1(c):
                moments(0, c, st1_sb, mv1_sb)

            def stats2(c):
                v.wait_ge(r2_sb, 2 * c + 2)
                stats(1, c, r2, st2_sb)

            def moments2(c):
                moments(1, c, st2_sb, mv2_sb)

            def normed(n, c, src, dst, row, rs_ready, done):
                v.wait_ge(rs_ready, c + 1)
                for s in range(S):
                    at = (c * 2 + n) * S + s
                    v.tensor_scalar(dst[:, (c * S + s) * row:(c * S + s) * row + D], src[:, s * D:(s + 1) * D],
                                    mv[:, at * 2:at * 2 + 1], rs[:, at:at + 1], ALU.subtract, ALU.mult).then_inc(done, 1)

            def norm1(c):
                normed(0, c, bank[3], x1, D, rs1_sb, x1_sb)

            def norm2(c):
                normed(1, c, r2, rows, RW, rs2_sb, x2_sb)

            def denominators(c):
                at = c * S
                v.wait_ge(xo_ps, c + 1)
                for h in range(2):
                    z = bank[5 + h][:].rearrange("p (s w) -> p s w", s=2)[:, :, D:D + 1]
                    v.tensor_scalar(den[:, at + 2 * h:at + 2 * h + 2].unsqueeze(2), z, EPS_X, None, ALU.add).then_inc(den_sb, 1)

            def den_reciprocal(c):
                v.wait_ge(den_sb, 2 * c + 2)
                v.reciprocal(chunk_of(rden, c, S), chunk_of(den, c, S)).then_inc(rden_sb, 1)

            def residual2(c):
                at = c * S
                if c:
                    v.wait_ge(x2_sb, S * c)
                v.wait_ge(rden_sb, c + 1)
                for h in range(2):
                    for n in range(2):
                        s = 2 * h + n
                        last = v.scalar_tensor_tensor(
                            r2[:, s * D:(s + 1) * D], bank[5 + h][:, n * 256:n * 256 + D],
                            rden[:, at + s:at + s + 1], tile_of(x1, c, s), ALU.mult, ALU.add)
                    last.then_inc(r2_sb, 1)

            W = S * E
            by_tile = lambda ap: ap.rearrange("p (s e) -> p s e", s=S)
            over_e = lambda ap: ap.unsqueeze(2).to_broadcast([P, S, E])
            lg = by_tile(bank[7][:, 0:W])

            def largest(c):
                v.wait_ge(lg_ps, c + 1)
                v.tensor_reduce(chunk_of(ltop, c, S), lg, X, ALU.max).then_inc(ltop_sb, 1)

            def is_largest(c):
                v.wait_ge(ltop_sb, c + 1)
                v.tensor_tensor(by_tile(chunk_of(leq, c, W)), lg, over_e(chunk_of(ltop, c, S)), ALU.is_equal).then_inc(leq_sb, 1)

            def first_keys(c):
                v.wait_ge(leq_sb, c + 1)
                v.tensor_tensor(by_tile(chunk_of(lcand, c, W)), by_tile(chunk_of(leq, c, W)),
                                rev[:].unsqueeze(1).to_broadcast([P, S, E]), ALU.mult).then_inc(lcand_sb, 1)

            def first_largest(c):
                v.wait_ge(lcand_sb, c + 1)
                v.tensor_reduce(chunk_of(lfirst, c, S), by_tile(chunk_of(lcand, c, W)), X, ALU.max).then_inc(lfirst_sb, 1)

            def one_hot(c):
                v.wait_ge(lfirst_sb, c + 1)
                v.tensor_tensor(by_tile(chunk_of(hot, c, W)), by_tile(chunk_of(lcand, c, W)),
                                over_e(chunk_of(lfirst, c, S)), ALU.is_equal).then_inc(hot_sb, 1)

            def place_rank(c):
                v.wait_ge(rank_ps, c + 1)
                v.tensor_tensor(by_tile(chunk_of(rk, c, W)), by_tile(bank[7][:, 0:W]),
                                region[:].unsqueeze(1).to_broadcast([P, S, E]), ALU.add).then_inc(rk_sb, 1)

            def place_hot(c):
                v.wait_ge(rk_sb, c + 1)
                v.tensor_tensor(chunk_of(rkh, c, W), chunk_of(rk, c, W), chunk_of(hot, c, W), ALU.mult).then_inc(rkh_sb, 1)

            def place(c):
                v.wait_ge(rkh_sb, c + 1)
                with nc.allow_low_precision(reason="row numbers are whole and under 2**24: exact in float32"):
                    v.tensor_reduce(chunk_of(pos, c, S), by_tile(chunk_of(rkh, c, W)), X, ALU.add).then_inc(pos_sb, 1)

            def shared_gated(c, h):
                v.wait_ge(sg_sb, 2 * c + h + 1)
                v.scalar_tensor_tensor(sg[:, h * CW:(h + 1) * CW], sg[:, h * CW:(h + 1) * CW], 1.0,
                                       bank[shared_banks(c, h)[0]][:], ALU.add, ALU.mult).then_inc(gated_sb, 1)

            def shared_hidden(c, h):
                if c >= 2:
                    v.wait_ge(sy_ps, c - 1)
                at = ((c % 2) * HALVES + h) * CW
                v.wait_ge(gated_sb, 2 * c + h + 1)
                v.tensor_tensor(hid[:, at:at + CW], sg[:, h * CW:(h + 1) * CW], bank[shared_banks(c, h)[1]][:], ALU.mult
                                ).then_inc(hid_sb, 1)

            def shared_out(c):
                v.wait_ge(sy_ps, c + 1)
                for h in range(2):
                    v.scalar_tensor_tensor(
                        rows_part(c, AT_BASE, D)[:, 2 * h:2 * h + 2, :],
                        bank[SHARED_OUT[c]][:, h * 2 * D:(h + 1) * 2 * D].rearrange("p (s d) -> p s d", s=2), 0.5,
                        rows_part(c, 0, D)[:, 2 * h:2 * h + 2, :], ALU.mult, ALU.add).then_inc(rowb_sb, 1)

            def context_copies():
                v.wait_ge(c_ps, 1)
                v.tensor_copy(proj_t[:], bank[5][:, 0:M]).then_inc(c_sb, 1)
                v.tensor_copy(ctx_t[:], bank[5][:, M:M + S * CTX]).then_inc(c_sb, 1)

            def context_scaled():
                v.wait_ge(kv_ps, 1)
                for n in range(2):
                    v.tensor_scalar(kvz[:, 2 * n * (D + 1):2 * (n + 1) * (D + 1)].rearrange("p (s w) -> p s w", s=2),
                                    bank[6 + n][0:M, :].rearrange("p (s w) -> p s w", s=2)[:, :, 0:D + 1],
                                    1.0 / math.sqrt(M), None, ALU.mult).then_inc(kv_sb, 1)

            scores(0, 1)
            context_copies()
            scores(0, 2)
            scores(0, 3)
            softmax_max(0)
            softmax_sub(0)
            softmax_sum(0)
            softmax_reciprocal(0)
            softmax_scale(0)
            attend(0, 1)
            attend(0, 2)
            scores(1, 1)
            attend(0, 3)
            scores(1, 2)
            scores(1, 3)
            softmax_max(1)
            softmax_sub(1)
            stats1(0)
            moments1(0)
            context_scaled()
            softmax_sum(1)
            norm1(0)
            softmax_reciprocal(1)
            softmax_scale(1)
            attend(1, 1)
            attend(1, 2)
            attend(1, 3)
            denominators(0)
            den_reciprocal(0)
            residual2(0)
            stats2(0)
            scores(2, 1)
            moments2(0)
            scores(2, 2)
            scores(2, 3)
            softmax_max(2)
            stats1(1)
            norm2(0)
            softmax_sub(2)
            moments1(1)
            softmax_sum(2)
            softmax_reciprocal(2)
            norm1(1)
            largest(0)
            softmax_scale(2)
            attend(2, 1)
            is_largest(0)
            first_keys(0)
            first_largest(0)
            attend(2, 2)
            one_hot(0)
            attend(2, 3)
            denominators(1)
            den_reciprocal(1)
            scores(3, 1)
            residual2(1)
            stats2(1)
            moments2(1)
            place_rank(0)
            place_hot(0)
            scores(3, 2)
            place(0)
            scores(3, 3)
            softmax_max(3)
            softmax_sub(3)
            norm2(1)
            stats1(2)
            shared_gated(0, 0)
            moments1(2)
            shared_hidden(0, 0)
            softmax_sum(3)
            softmax_reciprocal(3)
            largest(1)
            norm1(2)
            softmax_scale(3)
            is_largest(1)
            first_keys(1)
            attend(3, 1)
            attend(3, 2)
            first_largest(1)
            one_hot(1)
            shared_gated(0, 1)
            attend(3, 3)
            denominators(2)
            shared_hidden(0, 1)
            den_reciprocal(2)
            residual2(2)
            stats2(2)
            moments2(2)
            place_rank(1)
            place_hot(1)
            place(1)
            stats1(3)
            moments1(3)
            norm2(2)
            shared_out(0)
            norm1(3)
            largest(2)
            shared_gated(1, 0)
            is_largest(2)
            shared_hidden(1, 0)
            first_keys(2)
            first_largest(2)
            one_hot(2)
            shared_gated(1, 1)
            shared_hidden(1, 1)
            denominators(3)
            den_reciprocal(3)
            residual2(3)
            stats2(3)
            moments2(3)
            shared_gated(2, 0)
            place_rank(2)
            norm2(3)
            place_hot(2)
            place(2)
            shared_hidden(2, 0)
            shared_out(1)
            shared_gated(2, 1)
            shared_hidden(2, 1)
            shared_gated(3, 0)
            shared_hidden(3, 0)
            shared_gated(3, 1)
            shared_hidden(3, 1)
            shared_out(2)
            largest(3)
            is_largest(3)
            first_keys(3)
            first_largest(3)
            one_hot(3)
            place_rank(3)
            place_hot(3)
            place(3)

            step = [0]

            def tabled(ins):
                step[0] += 1
                ins.then_inc(tab, 1)
                v.wait_ge(tab, step[0])

            v.wait_ge(cnt_ps, 1)
            v.wait_ge(k_const, 2)
            tabled(v.tensor_copy(cnt[:], bank[6][0:1, 0:E]))
            tabled(v.tensor_tensor(tail_row[:], cnt[:], region[0:1, :], ALU.add))
            g3 = gtk[:].rearrange("p (e k) -> p e k", e=E)
            tabled(v.tensor_tensor(g3, cnt[:].unsqueeze(2).to_broadcast([1, E, KB]),
                                   kcol[:].unsqueeze(1).to_broadcast([1, E, KB]), ALU.is_gt))
            tabled(v.tensor_reduce(nblk[:], g3, X, ALU.add))
            m3 = nmask[:].rearrange("p (e f) -> p e f", e=E)
            tabled(v.tensor_tensor(m3, upto[:].rearrange("p (e f) -> p e f", e=E),
                                   nblk[:].unsqueeze(1).to_broadcast([1, E, E]), ALU.mult))
            tabled(v.tensor_reduce(cblk[:], m3, X, ALU.add))
            shared_out(3)
            tabled(v.tensor_scalar(dstep[:], nblk[:], -float(P), float(ROWS), ALU.mult, ALU.add))
            ge3 = ge[:].rearrange("p (b e) -> p b e", e=E)
            ged3 = ged[:].rearrange("p (b e) -> p b e", e=E)
            tabled(v.tensor_tensor(ge3, bcol[:].unsqueeze(2).to_broadcast([1, NBP, E]),
                                   cblk[:].unsqueeze(1).to_broadcast([1, NBP, E]), ALU.is_ge))
            tabled(v.tensor_tensor(ged3, ge3, dstep[:].unsqueeze(1).to_broadcast([1, NBP, E]), ALU.mult))
            tabled(v.tensor_reduce(rsum[:], ged3, X, ALU.add))
            tabled(v.scalar_tensor_tensor(radd[:], bcol[:], float(P), rsum[:], ALU.mult, ALU.add))
            tabled(v.tensor_scalar(blk_row[:], radd[:], float(FILLER), None, ALU.min))
            v.tensor_reduce(esum[:], ge3, X, ALU.add).then_inc(tab, 1)
            v.wait_ge(tab, TAB)
            v.tensor_scalar(blk_e[:], esum[:], float(E - 1), None, ALU.min).then_inc(tab, 1)
            def gated(b, q, r):
                v.wait_ge(si_sb, b + 1)
                v.scalar_tensor_tensor(ac[:, q * I:(q + 1) * I], bank[2 + q][:, I:2 * I],
                                       slots[:, r * RW + AT_SCORE:r * RW + AT_SCORE + 1], si[:, q * I:(q + 1) * I],
                                       ALU.mult, ALU.mult).then_inc(ac_sb, 1)

            def residual3(b, q, r, nth):
                v.wait_ge(y_ps, b + 1)
                if nth is not None:
                    v.wait_ge(out_dma[r], 16 * nth)
                v.tensor_copy(token[:, r:r + 1], slots[:, r * RW + AT_TOKEN:(r + 1) * RW].bitcast(I32))
                v.tensor_tensor(r3[:, r * D:(r + 1) * D], bank[6 + q][:, 0:D],
                                slots[:, r * RW + AT_BASE:r * RW + AT_BASE + D], ALU.add).then_inc(r3_sb, 1)

            def stats3(b, r):
                v.wait_ge(r3_sb, b + 1)
                v.bn_stats(st3[:, r * 6:(r + 1) * 6], r3[:, r * D:(r + 1) * D]).then_inc(st3_sb, 1)

            def aggr3(b, r):
                v.bn_aggr(mv3[:, 2 * r:2 * r + 2], st3[:, r * 6:(r + 1) * 6]).then_inc(mv3_sb, 1)

            def var3(b, r):
                v.wait_ge(mv3_sb, b + 1)
                v.tensor_scalar(ve3[:, r:r + 1], mv3[:, 2 * r + 1:2 * r + 2], EPS_LN, None, ALU.add).then_inc(ve3_sb, 1)

            def normed3(b, r):
                v.wait_ge(rs3_sb, b + 1)
                v.tensor_scalar(fin[:, r * D:(r + 1) * D], r3[:, r * D:(r + 1) * D], mv3[:, 2 * r:2 * r + 1],
                                rs3[:, r:r + 1], ALU.subtract, ALU.mult).then_inc(fin_sb, 1)

            def step3(b, r, nth, gate_next=True, norm_last=True):
                if gate_next:
                    gated(b + 2, r % 2, (r + 2) % RING)
                residual3(b, r % 2, r, nth)
                stats3(b, r)
                v.wait_ge(st3_sb, b + 1)
                if norm_last:
                    normed3(b - 1, (r - 1) % RING)
                aggr3(b, r)
                var3(b, r)

            gated(0, 0, 0)
            gated(1, 1, 1)
            for b in range(RING):
                step3(b, b, None, norm_last=b > 0)
            LOOPS = (NB - 5) // RING
            with v.Fori(0, LOOPS - 1) as k:
                for r in range(RING):
                    step3(RING * k + RING + r, r, k + 1)
            for b in range(RING * LOOPS, NB):
                step3(b, b % RING, b // RING, gate_next=b + 2 < NB)
            normed3(NB - 1, (NB - 1) % RING)

        @block.tensor
        def _(pe):
            pe.wait_ge(k_mask, 2)

            def weight_transposes():
                pe.wait_ge(ld_w, 64)
                pe.transpose(bank[4][:, 0:P], w_nat[:, 0:P], ident[:])
                for n in range(1, 4):
                    last = pe.transpose(bank[3][:, n * P:(n + 1) * P], w_nat[:, n * P:(n + 1) * P], ident[:])
                last.then_inc(w_ps, 1)

            def x0_transposes(c):
                pe.wait_ge(ld_x[c], 16)
                if c == 1:
                    pe.wait_ge(x0t_sb, 1)
                elif c > 1:
                    pe.wait_ge(att_t_sb, c - 1)
                for s in range(S):
                    last = pe.transpose(bank[0][:, s * D:(s + 1) * D], tile_of(x0, c, s), ident[:])
                last.then_inc(x0t_ps, 1)

            def project(c, s):
                pe.wait_ge(x0t_sb, c + 1)
                pe.wait_ge(w_sb, 2)
                n = S * c + s
                if n >= 2:
                    pe.wait_ge(qkv_sb, n - 1)
                pe.matmul(bank[1 + s % 2][:, 0:3 * D], tile_of(x0_t, c, s), w_t[:, 0:3 * D], start=True, stop=False)
                if n == 0:
                    pe.wait_ge(b3_sb, 6)
                    pe.wait_ge(k_spread, 4)
                pe.matmul(bank[1 + s % 2][:, 0:3 * D], spread[:], bias3[:, 0:3 * D], start=False, stop=True
                          ).then_inc(qkv_ps, 1)

            def att_transposes(c, first, last_i):
                pe.wait_ge(x0t_sb, min(c + 2, NC))
                pe.wait_ge(qkv_sb, S * c + 1)
                if first == 0:
                    v0 = qkv[:, c * S * 3 * D + 2 * D:c * S * 3 * D + 3 * D]
                    pe.matmul(bank[0][:, 0:D], v0, ident[:], start=True, stop=True)
                for i in range(max(first, 1), last_i + 1):
                    pe.wait_ge(pv_sb, 3 * c + i)
                    for j in range(i + 1):
                        at = (PB[i] + j) * D
                        last = pe.matmul(bank[0][:, i * D:(i + 1) * D], pv[:, at:at + D], ident[:],
                                         start=j == 0, stop=j == i)
                if last_i == S - 1:
                    last.then_inc(att_ps, 1)

            def att_out(c):
                pe.wait_ge(att_t_sb, c + 1)
                if c:
                    pe.wait_ge(x1_sb, S * c)
                for s in range(S):
                    o = bank[3][:, s * D:(s + 1) * D]
                    pe.matmul(o, att_t[:, s * D:(s + 1) * D], w_t[:, 3 * D:4 * D], start=True, stop=False)
                    pe.matmul(o, tile_of(x0_t, c, s), ident[:], start=False, stop=False)
                    last = pe.matmul(o, spread[:], bias3[:, 3 * D:4 * D], start=False, stop=True)
                last.then_inc(ao_ps, 1)

            def x1_transposes(c):
                if c:
                    pe.wait_ge(fq_sb, c)
                for s in range(S):
                    pe.wait_ge(x1_sb, S * c + s + 1)
                    last = pe.transpose(bank[4][:, s * D:(s + 1) * D], tile_of(x1, c, s), ident[:])
                last.then_inc(x1t_ps, 1)

            def features(c):
                pe.wait_ge(x1t_sb, c + 1)
                pe.matmul(bank[4][0:M, :], proj_t[:], x1_t[:], start=True, stop=True).then_inc(fq_ps, 1)

            def cross_out(c):
                pe.wait_ge(fq_sb, c + 1)
                if c:
                    pe.wait_ge(r2_sb, 2 * c)
                else:
                    pe.wait_ge(kv_sb, 2)
                for s in range(S):
                    last = pe.matmul(bank[5 + s // 2][:, (s % 2) * 256:(s % 2) * 256 + D + 1], rf_q[:, s * D:(s + 1) * D],
                                     kvz[:, s * (D + 1):(s + 1) * (D + 1)], start=True, stop=True)
                last.then_inc(xo_ps, 1)

            def x2_transposes(c):
                if c:
                    pe.wait_ge(pos_sb, c)
                for s in range(S):
                    pe.wait_ge(x2_sb, S * c + s + 1)
                    last = pe.transpose(bank[7][:, s * D:(s + 1) * D], tile_of(rows, c, s, D, RW), ident[:])
                last.then_inc(x2t_ps, 1)

            def logits(c):
                if c == 0:
                    pe.wait_ge(ld_gate, 16)
                pe.wait_ge(x2t_sb, c + 1)
                for s in range(S):
                    last = pe.matmul(bank[7][:, s * E:(s + 1) * E], tile_of(x2_t, c, s), gate[:], start=True, stop=True)
                last.then_inc(lg_ps, 1)

            def rank(c):
                pe.wait_ge(hot_sb, c + 1)
                if c:
                    pe.wait_ge(cum_sb, S * c)
                W = S * E
                o = bank[7][:, 0:W].rearrange("p (s e) -> p s e", s=S)
                pe.matmul(bank[7][:, 0:W], before[:], chunk_of(hot, c, W), start=True, stop=False)
                for s in range(S - 1):
                    tile_hot = hot[:, (c * S + s) * E:(c * S + s + 1) * E]
                    pe.matmul(o[:, s + 1:S, :], ones16[:], tile_hot.unsqueeze(1).to_broadcast([P, S - 1 - s, E]),
                              start=False, stop=False)
                pe.matmul(o, ones16[:], cum[:, c * E:(c + 1) * E].unsqueeze(1).to_broadcast([P, S, E]),
                          start=False, stop=True).then_inc(rank_ps, 1)

            def shared_up(c, h):
                g_bank, u_bank = shared_banks(c, h)
                pe.wait_ge(x2t_sb, c + 1)
                if (c, h) == (0, 0):
                    pe.wait_ge(ld_sh, 48)
                    pe.wait_ge(qkv_sb, NC * S)
                elif (c, h) == (1, 1):
                    pe.wait_ge(x1_sb, NC * S)
                    pe.wait_ge(rowb_sb, 2)
                elif c < 2:
                    pe.wait_ge(hid_sb, 2 * c + h)
                else:
                    pe.wait_ge(hid_sb, 2 * c + h - 1)
                pe.matmul(bank[u_bank][:], sh_gu[:, I + h * P:I + (h + 1) * P], chunk_of(x2_t, c, CW),
                          start=True, stop=True)
                pe.matmul(bank[g_bank][:], sh_gu[:, h * P:(h + 1) * P], chunk_of(x2_t, c, CW),
                          start=True, stop=True).then_inc(g_ps, 1)

            def shared_down(c):
                pe.wait_ge(hid_sb, 2 * c + 2)
                if c == 0:
                    pe.wait_ge(att_t_sb, NC)
                elif c == 1:
                    pe.wait_ge(fq_sb, NC)
                elif c == 2:
                    pe.wait_ge(r2_sb, 2 * NC)
                else:
                    pe.wait_ge(rowb_sb, 4)
                for s in range(S):
                    for h in range(HALVES):
                        at = ((c % 2) * HALVES + h) * CW + s * D
                        last = pe.matmul(bank[SHARED_OUT[c]][:, s * D:(s + 1) * D], hid[:, at:at + D],
                                         sh_dn[:, h * D:(h + 1) * D], start=h == 0, stop=h == HALVES - 1)
                last.then_inc(sy_ps, 1)

            def context_transposes():
                pe.wait_ge(ld_ctx, 16)
                pe.wait_ge(ld_proj, 16)
                pe.wait_ge(k_const, 1)
                pe.transpose(bank[5][:, 0:M], proj[:], ident[0:M, 0:M])
                c3 = ctx1[:].rearrange("p (s w) -> p s w", s=S)
                for s in range(S):
                    last = pe.transpose(bank[5][:, M + s * CTX:M + (s + 1) * CTX], c3[:, s, 0:D], ident[0:CTX, 0:CTX])
                last.then_inc(c_ps, 1)

            def context_features():
                pe.wait_ge(c_sb, 2)
                for s in range(S):
                    last = pe.matmul(bank[6][0:CTX, s * M:(s + 1) * M], ctx_t[:, s * CTX:(s + 1) * CTX], proj_t[:],
                                     start=True, stop=True)
                last.then_inc(fk_ps, 1)

            def context_sums():
                pe.wait_ge(fk_sb, 1)
                for s in range(S):
                    last = pe.matmul(bank[6 + s // 2][0:M, (s % 2) * 256:(s % 2) * 256 + D + 1],
                                     rf_k[:, s * M:(s + 1) * M],
                                     ctx1[:, s * (D + 1):(s + 1) * (D + 1)], start=True, stop=True)
                last.then_inc(kv_ps, 1)

            def count_tokens():
                pe.wait_ge(hot_sb, NC)
                pe.wait_ge(cum_sb, S * (NC - 1))
                pe.wait_ge(r2_sb, 2 * NC)
                pe.matmul(bank[6][:, 0:E], ones16[:], cum[:, (NC - 1) * E:NC * E], start=True, stop=False)
                for s in range(S):
                    at = ((NC - 1) * S + s) * E
                    last = pe.matmul(bank[6][:, 0:E], ones16[:], hot[:, at:at + E], start=False, stop=s == S - 1)
                last.then_inc(cnt_ps, 1)

            x0_transposes(0)
            weight_transposes()
            project(0, 0)
            project(0, 1)
            project(0, 2)
            project(0, 3)
            context_transposes()
            context_features()
            x0_transposes(1)
            context_sums()
            project(1, 0)
            project(1, 1)
            project(1, 2)
            att_transposes(0, 0, 1)
            att_transposes(0, 2, 2)
            att_transposes(0, 3, 3)
            project(1, 3)
            x0_transposes(2)
            att_out(0)
            project(2, 0)
            project(2, 1)
            project(2, 2)
            x1_transposes(0)
            project(2, 3)
            features(0)
            att_transposes(1, 0, 1)
            cross_out(0)
            att_transposes(1, 2, 2)
            att_transposes(1, 3, 3)
            att_out(1)
            x0_transposes(3)
            project(3, 0)
            project(3, 1)
            x2_transposes(0)
            project(3, 2)
            project(3, 3)
            logits(0)
            x1_transposes(1)
            features(1)
            rank(0)
            att_transposes(2, 0, 1)
            cross_out(1)
            att_transposes(2, 2, 2)
            shared_up(0, 0)
            att_transposes(2, 3, 3)
            att_out(2)
            x2_transposes(1)
            logits(1)
            shared_up(0, 1)
            x1_transposes(2)
            features(2)
            att_transposes(3, 0, 1)
            att_transposes(3, 2, 2)
            cross_out(2)
            att_transposes(3, 3, 3)
            rank(1)
            att_out(3)
            shared_down(0)
            x2_transposes(2)
            shared_up(1, 0)
            x1_transposes(3)
            logits(2)
            features(3)
            shared_up(1, 1)
            rank(2)
            cross_out(3)
            shared_up(2, 0)
            shared_up(2, 1)
            shared_down(1)
            x2_transposes(3)
            shared_up(3, 0)
            shared_up(3, 1)
            shared_down(2)
            logits(3)
            shared_down(3)
            rank(3)
            count_tokens()

            def turn(b, q, r, nth, reuse=True):
                pe.wait_ge(ld_slot[r], 16 * nth + 16)
                if reuse:
                    pe.wait_ge(xst_sb, b - 1)
                pe.transpose(bank[q][:, 0:D], slots[:, r * RW:r * RW + D], ident[:]).then_inc(xst_ps, 1)

            def experts_of(b, n):
                return nc.values_load_multi_w_load_instructions(
                    blk_e[0:1, ds(b, n)], engines=[mybir.EngineType.PE], min_val=0, max_val=E - 1,
                    skip_runtime_bounds_check_because="experts worked out on the chip, at most E - 1")[1]

            def up(b, q, ex, reuse=True):
                pe.wait_ge(xst_sb, b + 1)
                if reuse:
                    pe.wait_ge(ac_sb, b - 1)
                pe.matmul(bank[2 + q][:], xs_t[:, q * D:(q + 1) * D], rt_gu[:, ds(ex * (2 * I), 2 * I)],
                          start=True, stop=True).then_inc(gu_ps, 1)

            def turn_hidden(b, q, reuse=True):
                pe.wait_ge(ac_sb, b + 1)
                if reuse:
                    pe.wait_ge(act_sb, b - 1)
                for h in range(HALVES):
                    last = pe.transpose(bank[4 + q][:, h * P:(h + 1) * P], ac[:, q * I + h * P:q * I + (h + 1) * P], ident[:])
                last.then_inc(act_ps, 1)

            def down(b, q, ex, reuse=True):
                pe.wait_ge(act_sb, b + 1)
                if reuse:
                    pe.wait_ge(r3_sb, b - 1)
                for h in range(HALVES):
                    last = pe.matmul(bank[6 + q][:, 0:D], ac_t[:, q * I + h * P:q * I + (h + 1) * P],
                                     rt_dn[:, ds(ex * (HALVES * D) + h * D, D)], start=h == 0, stop=h == HALVES - 1)
                last.then_inc(y_ps, 1)

            pe.wait_ge(ld_rt, 48)
            pe.wait_ge(tab, TAB + 1)
            pe.wait_ge(rowb_sb, 2 * NC)
            def step(b, r, nth, ex, reuse=True):
                up(b, r % 2, ex[1])
                turn(b + 1, (r + 1) % 2, (r + 1) % RING, nth)
                down(b - 2, r % 2, ex[0], reuse)
                turn_hidden(b - 1, (r + 1) % 2, reuse)

            FIRST = 4
            ex = experts_of(0, FIRST)
            turn(0, 0, 0, 0, False)
            turn(1, 1, 1, 0, False)
            up(0, 0, ex[0], False)
            turn(2, 0, 2, 0)
            up(1, 1, ex[1], False)
            turn_hidden(0, 0, False)
            step(2, 2, 0, [ex[0], ex[2]], False)
            step(3, 3, 0, [ex[1], ex[3]], False)
            with pe.Fori(0, (NB - 5) // RING) as k:
                ex = experts_of(RING * k + FIRST - 2, RING + 2)
                for n in range(RING):
                    r = (FIRST + n) % RING
                    nth = k + (FIRST + n + 1) // RING
                    step(RING * k + (FIRST + n), r, nth, [ex[n], ex[n + 2]])
            ex = experts_of(NB - 3, 3)
            up(NB - 1, (NB - 1) % 2, ex[2])
            turn_hidden(NB - 2, (NB - 2) % 2)
            down(NB - 3, (NB - 3) % 2, ex[0])
            turn_hidden(NB - 1, (NB - 1) % 2)
            down(NB - 2, (NB - 2) % 2, ex[1])
            down(NB - 1, (NB - 1) % 2, ex[2])


_INS = ["x", "ctx_1024", "L0_attn_Wq", "L0_attn_bq", "L0_attn_Wk", "L0_attn_bk", "L0_attn_Wv", "L0_attn_bv",
        "L0_attn_Wo", "L0_attn_bo", "L0_attn_beta", "L0_xattn_projection", "L0_ffn_gate_w", "L0_ffn_sh_gate",
        "L0_ffn_sh_up", "L0_ffn_sh_down", "L0_ffn_rt_gate", "L0_ffn_rt_up", "L0_ffn_rt_down"]


def kernel(**inputs):
    import concourse.bacc as bacc
    from concourse.bass_utils import run_bass_kernel_spmd

    nc = bacc.Bacc("TRN2", target_bir_lowering=False, num_devices=1)
    arrays, t = {}, {}
    for name in _INS:
        a = np.ascontiguousarray(inputs[name])
        arrays[f"in_{name}"] = a
        t[name] = nc.dram_tensor(f"in_{name}", a.shape, mybir.dt.from_np(a.dtype), kind="ExternalInput").ap()
    t["out"] = nc.dram_tensor("out_x", inputs["x"].shape, mybir.dt.float32, kind="ExternalOutput").ap()
    build_decoder(nc, t)
    r = run_bass_kernel_spmd(nc, [arrays], core_ids=[0])
    return r.results[0]["out_x"]
```
